# Optimizing a Trainium2 kernel written in Bass

```python
import numpy as np
import jax
import jax.numpy as jnp

def _softmax(x, axis=-1):
    return jax.nn.softmax(x, axis=axis)

def _gelu(x):
    return jax.nn.gelu(x, approximate=True)

def _silu(x):
    return jax.nn.silu(x)

def _sigmoid(x):
    return jax.nn.sigmoid(x)

def _layernorm(x, axis=-1, eps=1e-05):
    m = jnp.mean(x, axis=axis, keepdims=True)
    v = jnp.var(x, axis=axis, keepdims=True)
    return (x - m) / jnp.sqrt(v + eps)

def _scatter_add(tgt, idx, src, axis=0):
    return tgt.at[idx].add(src)

def _segment_sum(src, seg, n):
    return jax.ops.segment_sum(src, seg, n)
kernel_name = 'mk_vit_tower_cls_d1_tok_img768_r4_be69f2'

def setup_inputs(seed: int=0):
    np.random.seed(seed)
    _w = jnp.asarray

    def _rec_inputs():
        import jax
        import jax.numpy as jnp
        _rk = jax.random.key(seed)
        x = -0.00016672 + 0.999947 * jax.random.normal(jax.random.fold_in(_rk, 1), (128, 3, 224, 224), jnp.float32)
        cls_tok = 0.02 * jax.random.normal(jax.random.fold_in(_rk, 5), (1, 1, 192), jnp.float32)
        return (x, cls_tok)
    x, cls_tok = _rec_inputs()

    def _L0_tok_setup():
        import jax, jax.numpy as jnp
        import numpy as np
        B, C, H, W = (64, 3, 96, 96)
        PS = 16
        PATCH_DIM = C * PS * PS
        EMBED_DIM = 192

        def patchify(x):
            b, c, h, w = x.shape
            n_p = h // PS
            p = x.reshape(b, c, n_p, PS, n_p, PS)
            p = p.transpose(0, 1, 2, 4, 3, 5)
            p = p.reshape(b, c, n_p * n_p, PS * PS)
            p = p.transpose(0, 2, 1, 3)
            return p.reshape(b, n_p * n_p, c * PS * PS)
        key = jax.random.key(seed)
        k1, k2, k3 = jax.random.split(key, 3)
        x = jax.random.normal(k1, (B, C, H, W), dtype=jnp.float32)
        scale = 1.0 / np.sqrt(PATCH_DIM)
        W_proj = jax.random.uniform(k2, (EMBED_DIM, PATCH_DIM), dtype=jnp.float32, minval=-scale, maxval=scale)
        b_proj = jax.random.uniform(k3, (EMBED_DIM,), dtype=jnp.float32, minval=-scale, maxval=scale)
        return {'x': x, 'W_proj': W_proj, 'b_proj': b_proj}
    _L0_tok_all = _L0_tok_setup()
    _L0_tok_in = {k: v for k, v in _L0_tok_all.items() if k in ('W_proj', 'b_proj')}
    del _L0_tok_all

    def _L0_attn_setup():
        import jax, jax.numpy as jnp
        import numpy as np
        SEQ_LEN = 1024
        EMB = 3
        FILTER_ORDER = 16
        CH = 192
        BATCH = 16
        SHIFT = 0.0
        MODULATE = True
        USE_BIAS = True
        FAST_DECAY_PCT = 0.3
        SLOW_DECAY_PCT = 1.5
        TARGET = 0.01

        def _pos_emb(L):
            t = jnp.linspace(0.0, 1.0, L)
            bands = (EMB - 1) // 2
            t_rescaled = jnp.linspace(0.0, float(L - 1), L)
            w = 2.0 * jnp.pi * t_rescaled / L
            f = jnp.linspace(0.0001, float(max(bands - 1, 0)), bands)
            z_c = jnp.exp(-1j * f[None, :] * w[:, None])
            z = jnp.concatenate([t[:, None], jnp.real(z_c), jnp.imag(z_c)], axis=-1)
            return (z.astype(jnp.float32), t.astype(jnp.float32))

        def _implicit_filter(L, w1, b1, w2, b2, w3, b3, freq, deltas_abs):
            z, t = _pos_emb(L)
            h = jnp.sin(freq * (z @ w1.T + b1))
            h = jnp.sin(freq * (h @ w2.T + b2))
            h = h @ w3.T + b3
            if MODULATE:
                decay = jnp.exp(-t[:, None] * deltas_abs[None, :])
                h = h * (decay + SHIFT)
            return h

        def fft_conv(u, k):
            seqlen = u.shape[-2]
            fft_size = 2 * seqlen
            u_f = jnp.fft.rfft(u.astype(jnp.float32), n=fft_size, axis=-2)
            k_f = jnp.fft.rfft(k.astype(jnp.float32), n=fft_size, axis=-2) / fft_size
            y = jnp.fft.irfft(u_f * k_f, n=fft_size, axis=-2)[..., :seqlen, :]
            return y.astype(u.dtype)
        key = jax.random.key(seed)
        ks = jax.random.split(key, 8)
        u = jax.random.normal(ks[0], (BATCH, SEQ_LEN, CH), dtype=jnp.float32)
        w1 = jax.random.normal(ks[1], (FILTER_ORDER, EMB), dtype=jnp.float32) * 0.5
        b1 = jax.random.normal(ks[2], (FILTER_ORDER,), dtype=jnp.float32) * 0.1
        w2 = jax.random.normal(ks[3], (FILTER_ORDER, FILTER_ORDER), dtype=jnp.float32) * 0.25
        b2 = jax.random.normal(ks[4], (FILTER_ORDER,), dtype=jnp.float32) * 0.1
        w3 = jax.random.normal(ks[5], (CH, FILTER_ORDER), dtype=jnp.float32) * 0.25
        b3 = jax.random.normal(ks[6], (CH,), dtype=jnp.float32) * 0.1
        freq = jnp.ones((FILTER_ORDER,), dtype=jnp.float32)
        max_decay = np.log(TARGET) / FAST_DECAY_PCT
        min_decay = np.log(TARGET) / SLOW_DECAY_PCT
        deltas_abs = jnp.abs(jnp.linspace(min_decay, max_decay, CH)).astype(jnp.float32)
        bias = jax.random.normal(ks[7], (CH,), dtype=jnp.float32)
        return {'u': u, 'w1': w1, 'b1': b1, 'w2': w2, 'b2': b2, 'w3': w3, 'b3': b3, 'freq': freq, 'deltas_abs': deltas_abs, 'bias': bias}
    _L0_attn_all = _L0_attn_setup()
    _L0_attn_in = {k: v for k, v in _L0_attn_all.items() if k in ('w1', 'b1', 'w2', 'b2', 'w3', 'b3', 'freq', 'deltas_abs', 'bias')}
    del _L0_attn_all

    def _L0_ffn_setup():
        import jax, jax.numpy as jnp
        import numpy as np
        B, T, E = (2, 256, 192)
        H = 768
        N_EXP = 4
        key = jax.random.key(seed)
        ks = jax.random.split(key, 8)
        s_e = 1.0 / np.sqrt(E)
        s_h = 1.0 / np.sqrt(H)
        return {'x': jax.random.normal(ks[0], (B, T, E), dtype=jnp.float32), 'Wg': jax.random.uniform(ks[1], (E, N_EXP), minval=-s_e, maxval=s_e, dtype=jnp.float32), 'bg': jax.random.uniform(ks[2], (N_EXP,), minval=-s_e, maxval=s_e, dtype=jnp.float32), 'W1': jax.random.uniform(ks[3], (N_EXP, E, H), minval=-s_e, maxval=s_e, dtype=jnp.float32), 'b1': jax.random.uniform(ks[4], (N_EXP, H), minval=-s_e, maxval=s_e, dtype=jnp.float32), 'W2': jax.random.uniform(ks[5], (N_EXP, H, E), minval=-s_h, maxval=s_h, dtype=jnp.float32), 'b2': jax.random.uniform(ks[6], (N_EXP, E), minval=-s_h, maxval=s_h, dtype=jnp.float32)}
    _L0_ffn_all = _L0_ffn_setup()
    _L0_ffn_in = {k: v for k, v in _L0_ffn_all.items() if k in ('Wg', 'bg', 'W1', 'b1', 'W2', 'b2')}
    del _L0_ffn_all
    return {'x': x, 'cls_tok': cls_tok, 'L0_tok_W_proj': _L0_tok_in['W_proj'], 'L0_tok_b_proj': _L0_tok_in['b_proj'], 'L0_attn_w1': _L0_attn_in['w1'], 'L0_attn_b1': _L0_attn_in['b1'], 'L0_attn_w2': _L0_attn_in['w2'], 'L0_attn_b2': _L0_attn_in['b2'], 'L0_attn_w3': _L0_attn_in['w3'], 'L0_attn_b3': _L0_attn_in['b3'], 'L0_attn_freq': _L0_attn_in['freq'], 'L0_attn_deltas_abs': _L0_attn_in['deltas_abs'], 'L0_attn_bias': _L0_attn_in['bias'], 'L0_ffn_Wg': _L0_ffn_in['Wg'], 'L0_ffn_bg': _L0_ffn_in['bg'], 'L0_ffn_W1': _L0_ffn_in['W1'], 'L0_ffn_b1': _L0_ffn_in['b1'], 'L0_ffn_W2': _L0_ffn_in['W2'], 'L0_ffn_b2': _L0_ffn_in['b2']}

def reference(x, cls_tok, L0_tok_W_proj, L0_tok_b_proj, L0_attn_w1, L0_attn_b1, L0_attn_w2, L0_attn_b2, L0_attn_w3, L0_attn_b3, L0_attn_freq, L0_attn_deltas_abs, L0_attn_bias, L0_ffn_Wg, L0_ffn_bg, L0_ffn_W1, L0_ffn_b1, L0_ffn_W2, L0_ffn_b2):
    import jax
    import jax.numpy as jnp

    def _L0_tok_ref(x, W_proj, b_proj):
        import jax, jax.numpy as jnp
        import numpy as np
        B, C, H, W = (64, 3, 96, 96)
        PS = 16
        PATCH_DIM = C * PS * PS
        EMBED_DIM = 192

        def patchify(x):
            b, c, h, w = x.shape
            n_p = h // PS
            p = x.reshape(b, c, n_p, PS, n_p, PS)
            p = p.transpose(0, 1, 2, 4, 3, 5)
            p = p.reshape(b, c, n_p * n_p, PS * PS)
            p = p.transpose(0, 2, 1, 3)
            return p.reshape(b, n_p * n_p, c * PS * PS)
        patches = patchify(x)
        return jnp.einsum('bnd,ed->bne', patches, W_proj) + b_proj

    def _L0_attn_ref(u, w1, b1, w2, b2, w3, b3, freq, deltas_abs, bias):
        import jax, jax.numpy as jnp
        import numpy as np
        SEQ_LEN = 1024
        EMB = 3
        FILTER_ORDER = 16
        CH = 192
        BATCH = 16
        SHIFT = 0.0
        MODULATE = True
        USE_BIAS = True
        FAST_DECAY_PCT = 0.3
        SLOW_DECAY_PCT = 1.5
        TARGET = 0.01

        def _pos_emb(L):
            t = jnp.linspace(0.0, 1.0, L)
            bands = (EMB - 1) // 2
            t_rescaled = jnp.linspace(0.0, float(L - 1), L)
            w = 2.0 * jnp.pi * t_rescaled / L
            f = jnp.linspace(0.0001, float(max(bands - 1, 0)), bands)
            z_c = jnp.exp(-1j * f[None, :] * w[:, None])
            z = jnp.concatenate([t[:, None], jnp.real(z_c), jnp.imag(z_c)], axis=-1)
            return (z.astype(jnp.float32), t.astype(jnp.float32))

        def _implicit_filter(L, w1, b1, w2, b2, w3, b3, freq, deltas_abs):
            z, t = _pos_emb(L)
            h = jnp.sin(freq * (z @ w1.T + b1))
            h = jnp.sin(freq * (h @ w2.T + b2))
            h = h @ w3.T + b3
            if MODULATE:
                decay = jnp.exp(-t[:, None] * deltas_abs[None, :])
                h = h * (decay + SHIFT)
            return h

        def fft_conv(u, k):
            seqlen = u.shape[-2]
            fft_size = 2 * seqlen
            u_f = jnp.fft.rfft(u.astype(jnp.float32), n=fft_size, axis=-2)
            k_f = jnp.fft.rfft(k.astype(jnp.float32), n=fft_size, axis=-2) / fft_size
            y = jnp.fft.irfft(u_f * k_f, n=fft_size, axis=-2)[..., :seqlen, :]
            return y.astype(u.dtype)
        L = u.shape[-2]
        k = _implicit_filter(L, w1, b1, w2, b2, w3, b3, freq, deltas_abs)
        y = fft_conv(u, k)
        if USE_BIAS:
            y = y + u * bias
        return y

    def _L0_ffn_ref(x, Wg, bg, W1, b1, W2, b2):
        import jax, jax.numpy as jnp
        import numpy as np
        B, T, E = (2, 256, 192)
        H = 768
        N_EXP = 4
        gate_logits = jnp.einsum('bte,en->btn', x, Wg) + bg
        top = jnp.argmax(gate_logits, axis=-1)
        h = jax.nn.gelu(jnp.einsum('bte,neh->nbth', x, W1) + b1[:, None, None, :], approximate=False)
        y = jnp.einsum('nbth,nhe->nbte', h, W2) + b2[:, None, None, :]
        onehot = jax.nn.one_hot(top, N_EXP, dtype=x.dtype)
        out = jnp.einsum('nbte,btn->bte', y, onehot)
        return out
    h = _L0_tok_ref(x, L0_tok_W_proj, L0_tok_b_proj)
    h = jnp.concatenate([jnp.broadcast_to(cls_tok, (h.shape[0], 1, h.shape[2])), h], axis=1)
    h = h + _L0_attn_ref(_layernorm(h, axis=-1), L0_attn_w1, L0_attn_b1, L0_attn_w2, L0_attn_b2, L0_attn_w3, L0_attn_b3, L0_attn_freq, L0_attn_deltas_abs, L0_attn_bias)
    h = h + _L0_ffn_ref(_layernorm(h, axis=-1), L0_ffn_Wg, L0_ffn_bg, L0_ffn_W1, L0_ffn_b1, L0_ffn_W2, L0_ffn_b2)
    return h

_drawn_inputs = setup_inputs


def setup_inputs(seed=0):
    import zlib

    import numpy as np

    out = dict(_drawn_inputs(seed))
    spreads = {'L0_attn_freq': (1.0, 0.6)}
    factors = {'L0_attn_w1': 18.589,
     'L0_attn_b1': 26.782,
     'L0_attn_w2': 47.408,
     'L0_attn_b2': 65.865,
     'L0_attn_w3': 16.861,
     'L0_attn_b3': 53.464,
     'L0_attn_deltas_abs': 200.0,
     'L0_ffn_b1': 4.427,
     'L0_ffn_b2': 3.041}
    for name, (base, spread) in spreads.items():
        noise = np.random.default_rng([zlib.crc32(name.encode()), seed]).standard_normal(out[name].shape)
        drawn = base * np.exp(spread * noise) if base else spread * noise
        out[name] = jnp.asarray(drawn.astype(out[name].dtype))
    for name, factor in factors.items():
        out[name] = (out[name] * factor).astype(out[name].dtype)
    return out
```

```python
from contextlib import ExitStack
import math

import concourse.bass as bass
from concourse import mybir

P = 128
F32 = mybir.dt.float32
F16 = mybir.dt.float16
I32 = mybir.dt.int32
ALU = mybir.AluOpType
ACT = mybir.ActivationFunctionType
AX_X = mybir.AxisListType.X

B, IC, IMG = 128, 3, 224
PS = 16
G = IMG // PS
L = 1 + G * G
D = 192
E = 4
HID = 768
FO = 16
EPS = 1e-5

KC = IC * PS * PS // P
ROWS = 8
CHUNK = ROWS * IMG
HALF = G // 2
HT = HALF * P

CG = 4
NCG = D // CG
L1 = L - P
PADDED = P - 1 + L
SKEW_SLOTS = 4

ROW = 196
STAT0, STAT1, TOKEN = 192, 193, 194

TS = 256
NB = HID // P
WAVES = (74, 123)
TG = 4
PB = 2 * D // P
AHEAD = 6
WSCALE = 64.0
LOW = 64
NOWHERE = 1 << 20
MAGIC = 1.5 * 2.0 ** 23
WAVE_TILES = tuple((n * P + E * (TS - 1)) // TS for n in WAVES)
NT = sum(WAVE_TILES)
W1F = E * HID
W2F = E * NB * D
WF = 2 * W1F + W2F
SEND, SEND_FIRST = 4, 6
assert SEND_FIRST + SEND * WAVE_TILES[0] >= 2 * WAVE_TILES[1]
assert sum(WAVES) == L and WAVE_TILES[0] % 4 == 0 and TG % 2 == 0


def vit_block(nc, x, cls_tok, wprojT, b_proj, zT, trow, fw1T, fw2T, fw3T, fcols, f3cols,
              w_gate, b_gate, w1, b1c, w2, b2, ident_d, triu_d, tokno_d, padno_d, tileno_d, out):
    kpad = nc.dram_tensor("kpad", (D, PADDED), F32).ap()
    wsplit = nc.dram_tensor("wsplit", (P, 2 * WF), F16).ap()
    rows = nc.dram_tensor("rows", (NT * TS, ROW), F32).ap()
    out_rows = out.rearrange("b t c -> (b t) c")
    x_chunks = x.rearrange("b c (r y) w -> b c r (y w)", y=ROWS)

    with ExitStack() as whole:
        def sem(name):
            return whole.enter_context(nc.semaphore(name))

        def sb(stack, name, shape, dt=F32):
            return stack.enter_context(nc.sbuf_tensor(name, shape, dt))

        H = sb(whole, "H", [P, L, ROW])
        ident = sb(whole, "ident", [P, P])
        Hflat = H[:, :, :].rearrange("p t c -> p (t c)")

        stage_a(nc, sem, sb, H, Hflat, ident, x_chunks, cls_tok, wprojT, b_proj, zT, trow, fw1T, fw2T,
                fw3T, fcols, f3cols, w1, w2, ident_d, kpad, wsplit)
        stage_b(nc, sem, sb, H, ident, kpad)
        stage_c(nc, sem, sb, H, Hflat, ident, w_gate, b_gate, b1c, b2, triu_d, tokno_d, padno_d, tileno_d,
                wsplit, rows, out_rows)


def stage_a(nc, sem, sb, H, Hflat, ident, x_chunks, cls_tok, wprojT, b_proj, zT, trow, fw1T, fw2T, fw3T,
            fcols, f3cols, w1, w2, ident_d, kpad, wsplit):
    with ExitStack() as st:
        xr = sb(st, "xr", [P, KC, CHUNK])
        xh = sb(st, "xh", [P, 2, HT], F16)
        xl = sb(st, "xl", [P, 2, HT], F16)
        wp = sb(st, "wp", [P, 2, KC, D], F16)
        bp = sb(st, "bp", [P, D])
        bn = sb(st, "bn", [P, HALF, 6])
        tp = [st.enter_context(nc.psum_tensor(f"tp{i}", [P, 1024], F32)) for i in range(2)]
        acc = st.enter_context(nc.psum_tensor("acc", [P, 8, 256], F32))

        tail = (L - HALF) * ROW
        base = tail - 2 * WF
        w_raw = Hflat[:, base:base + WF]
        w_hl = Hflat[:, base + WF:base + 2 * WF].bitcast(F16).rearrange("p (h f) -> p h f", h=2)
        at = [48 * ROW]

        def stage(parts, n):
            v = Hflat[0:parts, at[0]:at[0] + n]
            at[0] += n
            return v

        wp_raw = stage(P, KC * D).rearrange("p (k e) -> p k e", k=KC)
        xp_b = sb(st, "xp_b", [P, 4 * P])
        xp = ((Hflat[:, tail:tail + 4 * P], Hflat[:, tail + 4 * P:tail + 7 * P]),
              (xp_b[:, :], Hflat[:, tail + 7 * P:tail + 10 * P]))
        z_s, t_s = stage(3, L), stage(96, L)
        fw1_s, fw2_s, fw3_s = stage(3, FO), stage(FO, FO), stage(FO, D)
        fc = stage(FO, 4)
        f3 = stage(96, 8)
        ang, nr, nf, hid = stage(FO, L), stage(FO, L), stage(FO, L), stage(FO, L)
        decay = stage(96, 2 * L).rearrange("p (h t) -> p h t", h=2)
        kp = stage(96, 2 * PADDED).rearrange("p (h t) -> p h t", h=2)

        consts_in, wraw_in, cls_in, kpad_out, wsplit_out = (
            sem(s) for s in ("consts_in", "wraw_in", "cls_in", "kpad_out", "wsplit_out"))
        chunk_in = [sem(f"chunk_in{k}") for k in range(KC)]
        f_mm, f_dve, f_act, wsp_hi, wsp_lo = (sem(s) for s in ("f_mm", "f_dve", "f_act", "wsp_hi", "wsp_lo"))
        turned, high, low, half_acc, bn_done, stats_done = (
 sem(s) for s in ("turned", "high", "low", "half_acc", "bn_done", "stats_done"))
        half_out = [sem(f"half_out{c}") for c in range(2)]
        ordered = [sem(f"ordered{c}") for c in range(2)]

        block = st.enter_context(nc.Block())

        def patches(n, c):
            g0, g1 = n // KC * HALF + 4 * c, n // KC * HALF + (4, HALF)[c]
            return (xp[n % 2][c].rearrange("p (g y w) -> p g y w", y=ROWS, w=PS),
                    xr[:, n % KC, :].rearrange("p (y g w) -> p g y w", y=ROWS, w=PS)[:, g0:g1, :, :])

        @block.sync
        def _(sp):
            sp.dma_start(ident[:, :], ident_d).then_inc(consts_in, 16)
            for dst, src in ((z_s, zT), (t_s, trow.partition_broadcast(96)), (fw1_s, fw1T), (fw2_s, fw2T),
                             (fw3_s, fw3T), (fc, fcols), (f3[:, 0:6], f3cols)):
                sp.dma_start(dst, src).then_inc(consts_in, 16)
            sp.dma_start(bp[:, :], b_proj.partition_broadcast(P)).then_inc(consts_in, 16)
            sp.dma_start(wp_raw, wprojT.rearrange("(k p) e -> p k e", p=P)).then_inc(consts_in, 16)
            for k in range(KC):
                sp.dma_start(xr[:, k, :], x_chunks[:, k // 2, k % 2, :]).then_inc(chunk_in[k], 16)
            with sp.Fori(1, G) as gy:
                for k in range(KC):
                    for c in range(2):
                        sp.wait_ge(ordered[c], 2 * KC * gy - KC + k + 1)
                    sp.dma_start(xr[:, k, :], x_chunks[:, k // 2, bass.ds(2 * gy + k % 2, 1), :]
                                 .rearrange("b o w -> b (o w)")).then_inc(chunk_in[k], 16)
            sp.wait_ge(kpad_out, 16)
            sp.wait_ge(wsplit_out, 16)

        @block.scalar
        def _(act):
            act.dma_start(H[:, 0, 0:D], cls_tok.partition_broadcast(P)).then_inc(cls_in, 16)
            act.dma_start(w_raw[:, 0:W1F].rearrange("p (e h) -> p e h", e=E),
                          w1[:, 0:P, :].rearrange("e c h -> c e h")).then_inc(wraw_in, 16)
            for s in range(2):
                act.dma_start(w_raw[s * LOW:(s + 1) * LOW, W1F:2 * W1F].rearrange("p (e h) -> p e h", e=E),
                              w1[:, P:D, :].rearrange("e c h -> c e h")).then_inc(wraw_in, 16)
            act.dma_start(w_raw[:, 2 * W1F:WF].rearrange("p (k c) -> p k c", c=D),
                          w2.rearrange("e (k p) c -> p (e k) c", p=P)).then_inc(wraw_in, 16)
            act.wait_ge(consts_in, 16 * 10)
            act.activation(wp[:, 0, :, :], wp_raw, ACT.Copy, scale=WSCALE).then_inc(wsp_hi, 1)
            for n in range(2):
                act.wait_ge(f_dve, 7 * n + 7)
                act.activation(hid, ang, ACT.Sin).then_inc(f_act, 1)
            act.wait_ge(f_dve, 15)
            for h in range(2):
                act.activation(decay[:, h, :], t_s, ACT.Exp, scale=f3[:, 6 + h:7 + h]).then_inc(f_act, 1)
            act.wait_ge(wraw_in, 64)
            act.activation(w_hl[:, 0, :], w_raw, ACT.Copy, scale=WSCALE).then_inc(wsp_hi, 1)
            act.wait_ge(wsp_lo, 2)
            act.dma_start(wsplit, w_hl.rearrange("p h f -> p (h f)")).then_inc(wsplit_out, 16)
            def high_part(n, q):
                act.wait_ge(turned, q + 1)
                wait(act, half_acc, 2 * (q - 1))
                act.activation(xh[:, n % 2, :], tp[n % 2][:, 0:HT], ACT.Copy).then_inc(high, 1)

            def order(n, gy, q):
                act.wait_ge(chunk_in[n % KC], 16 * (gy + 1))
                wait(act, turned, q - 1)
                dst, src = patches(n, 0)
                act.activation(dst, src, ACT.Copy).then_inc(ordered[0], 1)

            order(0, 0, 0)
            order(1, 0, 1)
            for n in range(2 * KC):
                high_part(n, n)
                order((n + 2) % (2 * KC), (n + 2) // (2 * KC), n + 2)
            with act.Fori(1, G - 1) as gy:
                for n in range(2 * KC):
                    high_part(n, 2 * KC * gy + n)
                    order((n + 2) % (2 * KC), gy + (n + 2) // (2 * KC), 2 * KC * gy + n + 2)
            for n in range(2 * KC):
                high_part(n, 2 * KC * (G - 1) + n)
                if n + 2 < 2 * KC:
                    order(n + 2, G - 1, 2 * KC * (G - 1) + n + 2)

        @block.tensor
        def _(pe):
            pe.wait_ge(consts_in, 16 * 10)
            pe.matmul(tp[0][0:FO, 0:L], fw1_s, z_s, start=True, stop=True).then_inc(f_mm, 1)
            pe.wait_ge(f_act, 1)
            pe.matmul(tp[1][0:FO, 0:L], fw2_s, hid, start=True, stop=True).then_inc(f_mm, 1)
            pe.wait_ge(f_act, 2)
            for h in range(2):
                pe.matmul(tp[0][0:96, 512 * h:512 * h + L], fw3_s[:, 96 * h:96 * h + 96], hid,
                          start=True, stop=True).then_inc(f_mm, 1)
            pe.wait_ge(f_dve, 18)
            pe.wait_ge(wsp_lo, 1)

            def turn(n, q):
                for c in range(2):
                    pe.wait_ge(ordered[c], q + 1)
                wait(pe, high, q - 1)
                wait(pe, low, q - 1)
                for i in range(HALF):
                    piece = xp[n % 2][i // 4]
                    mm = pe.transpose(tp[n % 2][:, i * P:(i + 1) * P], piece[:, i % 4 * P:i % 4 * P + P], ident[:, :])
                mm.then_inc(turned, 1)

            def project(n, q, hn):
                k, s = n % KC, n % 2
                pe.wait_ge(high, q + 1)
                pe.wait_ge(low, q + 1)
                for i in range(HALF):
                    if k == 0 and i in (0, 4):
                        pe.wait_ge(half_out[i // 4], hn)
                    t = slice(i * P, (i + 1) * P)
                    o = acc[:, i, 0:D]
                    pe.matmul(o, xh[:, s, t], wp[:, 0, k, :], start=(k == 0 and i % 2 == 0), stop=False,
                              skip_group_check=True)
                    pe.matmul(o, xh[:, s, t], wp[:, 1, k, :], start=False, stop=False, skip_group_check=True)
                    mm = pe.matmul(o, xl[:, s, t], wp[:, 0, k, :], start=False, stop=(k == KC - 1),
                                   skip_group_check=True)
                    if i in (3, HALF - 1):
                        mm.then_inc(half_acc, 1)

            turn(0, 0)
            with pe.Fori(0, G - 1) as gy:
                for n in range(2 * KC):
                    q = 2 * KC * gy + n
                    if n + 1 < 2 * KC:
                        turn(n + 1, q + 1)
                    else:
                        turn(0, q + 1)
                    project(n, q, 2 * gy + n // KC)
            gy = G - 1
            for n in range(2 * KC):
                q = 2 * KC * gy + n
                if n + 1 < 2 * KC:
                    turn(n + 1, q + 1)
                project(n, q, 2 * gy + n // KC)

        @block.vector
        def _(dve):
            nd = [0]

            def f_step(ins):
                ins.then_inc(f_dve, 1)
                nd[0] += 1
                dve.wait_ge(f_dve, nd[0])

            dve.wait_ge(consts_in, 16 * 10)
            dve.wait_ge(wsp_hi, 1)
            dve.scalar_tensor_tensor(wp[:, 1, :, :], wp_raw, WSCALE, wp[:, 0, :, :], ALU.mult,
                                     ALU.subtract).then_inc(wsp_lo, 1)
            for n in range(2):
                dve.wait_ge(f_mm, n + 1)
                f_step(dve.tensor_scalar(ang, tp[n][0:FO, 0:L], fc[:, n:n + 1], fc[:, 2:3], ALU.add, ALU.mult))
                f_step(dve.tensor_scalar(nr, ang, 1 / (2 * math.pi), MAGIC, ALU.mult, ALU.add))
                f_step(dve.tensor_scalar(nf, nr, MAGIC, None, ALU.subtract))
                rest = 2 * math.pi
                for bits in (7, 17, 30):
                    part = round(rest * 2 ** bits) / 2 ** bits
                    rest -= part
                    f_step(dve.scalar_tensor_tensor(ang, nf, -part, ang, ALU.mult, ALU.add))
                f_step(dve.tensor_scalar(ang, ang, 3.1415925, -3.1415925, ALU.min, ALU.max))
            f_step(dve.tensor_scalar(f3[:, 6:8], f3[:, 2:4], -1.0, None, ALU.mult))
            f_step(dve.memset(kp, 0.0))
            for h in range(2):
                dve.wait_ge(f_mm, 3 + h)
                dve.wait_ge(f_act, 3 + h)
                dve.scalar_tensor_tensor(kp[:, h, P - 1:PADDED], tp[0][0:96, 512 * h:512 * h + L], f3[:, h:h + 1],
                                         decay[:, h, :], ALU.add, ALU.mult).then_inc(f_dve, 1)
                nd[0] += 1
            dve.wait_ge(f_dve, nd[0])
            f_step(dve.tensor_scalar(kp[:, :, P - 1:PADDED], kp[:, :, P - 1:PADDED], 1.0 / (2 * L), None, ALU.mult))
            f_step(dve.tensor_tensor(kp[:, :, P - 1], kp[:, :, P - 1], f3[:, 4:6], ALU.add))
            dve.wait_ge(wsp_hi, 2)
            dve.scalar_tensor_tensor(w_hl[:, 1, :], w_raw, WSCALE, w_hl[:, 0, :], ALU.mult,
                                     ALU.subtract).then_inc(wsp_lo, 1)
            def pairs(v):
                return v.rearrange("p t (h s) -> p t h s", h=2)[:, :, :, 1:3]

            dve.wait_ge(cls_in, 16)
            dve.bn_stats(bn[:, 0, :], H[:, 0, 0:D]).then_inc(bn_done, 1)
            dve.wait_ge(bn_done, 1)
            dve.tensor_copy(H[:, 0:1, D:D + 4], pairs(bn[:, 0:1, :])).then_inc(stats_done, 1)
            dve.wait_ge(stats_done, 1)

            def low_part(n, q):
                dve.wait_ge(high, q + 1)
                dve.tensor_tensor(xl[:, n % 2, :], tp[n % 2][:, 0:HT], xh[:, n % 2, :], ALU.subtract).then_inc(low, 1)

            def tokens_out(hn, t0):
                for i0, i1, c in ((0, 4, 1), (4, HALF, 2)):
                    dve.wait_ge(half_acc, 2 * KC * (hn + 1) - 2 + c)
                    dve.scalar_tensor_tensor(
                        H[:, bass.ds(t0 + i0, i1 - i0), 0:D], acc[:, i0:i1, 0:D], 1 / WSCALE,
                        bp[:, :].rearrange("p (o e) -> p o e", o=1).to_broadcast([P, i1 - i0, D]),
                        ALU.mult, ALU.add).then_inc(half_out[c - 1], 1)

            def statistics(hn, i0, i1):
                waits(dve, (cls_in, 16), (half_out[0], hn + 1), (half_out[1], hn + 1),
                      (stats_done, (len(SHARE) - 1) * hn + SHARE.index(i0) + 1))
                for i in range(i0, i1):
                    dve.bn_stats(bn[:, i, :], H[:, bass.ds(1 + HALF * hn + i, 1), 0:D].rearrange("p o c -> p (o c)")
                                 ).then_inc(bn_done, 1)
                dve.wait_ge(bn_done, HALF * hn + i1 + 1)
                dve.tensor_copy(H[:, bass.ds(1 + HALF * hn + i0, i1 - i0), D:D + 4], pairs(bn[:, i0:i1, :])
                                ).then_inc(stats_done, 1)

            SHARE = (0, 2, 3, 5, 6, 7)

            def half_steps(half, hn, first=False, last=False):
                q0 = KC * hn
                for k in range(1, KC):
                    low_part(half * KC + k, q0 + k)
                    if not first:
                        statistics(hn - 1, SHARE[k - 1], SHARE[k])
                if not last:
                    low_part(half * KC + KC, q0 + KC)
                tokens_out(hn, 1 + HALF * hn)

            low_part(0, 0)
            half_steps(0, 0, first=True)
            half_steps(1, 1)
            for g0, g1 in ((1, 3), (3, G - 1)):
                if g0 == 3:
                    dve.wait_ge(kpad_out, 16)
                    dve.wait_ge(wsplit_out, 16)
                with dve.Fori(g0, g1) as gy:
                    for half in range(2):
                        half_steps(half, 2 * gy + half)
            for half in range(2):
                half_steps(half, 2 * (G - 1) + half, last=half == 1)
            for k in range(1, KC):
                statistics(2 * G - 1, SHARE[k - 1], SHARE[k])
            dve.wait_ge(stats_done, 2 * G * (len(SHARE) - 1) + 1)

        @block.gpsimd
        def _(pool):
            def order(n, gy, q):
                waits(pool, (consts_in, 16 * 10), (chunk_in[n % KC], 16 * (gy + 1)), (turned, q - 1))
                dst, src = patches(n, 1)
                pool.tensor_copy(dst, src).then_inc(ordered[1], 1)

            order(0, 0, 0)
            order(1, 0, 1)
            pool.wait_ge(f_dve, 20)
            pool.dma_start(kpad.rearrange("(h p) l -> p h l", h=2), kp).then_inc(kpad_out, 16)
            for n in range(2, 2 * KC):
                order(n, 0, n)
            with pool.Fori(1, G) as gy:
                for n in range(2 * KC):
                    order(n, gy, 2 * KC * gy + n)
            pool.wait_ge(kpad_out, 16)


def stage_b(nc, sem, sb, H, ident, kpad):
    with ExitStack() as st:
        m1 = sb(st, "m1", [P, L])
        v1 = sb(st, "v1", [P, L])
        rs = sb(st, "rs", [P, L])
        t1 = sb(st, "t1", [P, L])
        dif = sb(st, "dif", [P, 2, CG, L])
        u = sb(st, "u", [P, 2, CG, L])
        uT0 = sb(st, "uT0", [P, 2, CG * P])
        uT1 = sb(st, "uT1", [L1, 2, CG * P])
        skew = sb(st, "skew", [P, SKEW_SLOTS, CG, L])
        tp0 = st.enter_context(nc.psum_tensor("tp0b", [P, 2, 512], F32))
        tp1 = st.enter_context(nc.psum_tensor("tp1b", [L1, 2, 512], F32))
        yps = st.enter_context(nc.psum_tensor("yps", [P, 2, CG, 256], F32))
        skew_in = [sem(f"skew_in{i}") for i in range(SKEW_SLOTS)]
        ln1, ln1_sqrt, centred, normed, turned, evac0, conv, added = (
            sem(s) for s in ("ln1", "ln1_sqrt", "b_centred", "b_normed", "b_turned", "b_evac", "b_conv", "b_added"))
        Hc = H[:, :, :].rearrange("p t c -> p c t")
        block = st.enter_context(nc.Block())

        def skew_dma(sp, g, s):
            src = kpad[bass.ds(CG * g, CG), 0:L]
            src = bass.AP(src.tensor, src.offset, [[1, P], [PADDED, CG], [1, L]])
            sp.dma_start(skew[:, s, :, :], src).then_inc(skew_in[s], 16)

        @block.sync
        def _(sp):
            for s in range(SKEW_SLOTS):
                skew_dma(sp, s, s)
            with sp.Fori(1, NCG // SKEW_SLOTS) as it:
                for s in range(SKEW_SLOTS):
                    g = it * SKEW_SLOTS + s
                    sp.wait_ge(conv, g - SKEW_SLOTS + 1)
                    skew_dma(sp, g, s)

        @block.vector
        def _(dve):
            n = [0]

            def step(ins):
                ins.then_inc(ln1, 1)
                n[0] += 1
                dve.wait_ge(ln1, n[0])

            m_even, s_even, m_odd, s_odd = (H[:, :, D + c] for c in range(4))
            step(dve.tensor_tensor(m1[:, :], m_even, m_odd, ALU.add))
            step(dve.tensor_scalar(m1[:, :], m1[:, :], 0.5, None, ALU.mult))
            step(dve.tensor_tensor(t1[:, :], m_even, m_odd, ALU.subtract))
            step(dve.scalar_tensor_tensor(t1[:, :], t1[:, :], 0.25 * D, t1[:, :], ALU.mult, ALU.mult))
            step(dve.tensor_tensor(v1[:, :], s_even, s_odd, ALU.add))
            step(dve.tensor_tensor(v1[:, :], v1[:, :], t1[:, :], ALU.add))
            step(dve.tensor_scalar(v1[:, :], v1[:, :], 1.0 / D, EPS, ALU.mult, ALU.add))
            dve.wait_ge(ln1_sqrt, 1)
            step(dve.reciprocal(rs[:, :], t1[:, :]))
            step(dve.tensor_tensor(t1[:, :], rs[:, :], rs[:, :], ALU.mult))
            step(dve.tensor_tensor(t1[:, :], t1[:, :], v1[:, :], ALU.mult))
            step(dve.tensor_scalar(t1[:, :], t1[:, :], -0.5, 1.5, ALU.mult, ALU.add))
            step(dve.tensor_tensor(rs[:, :], rs[:, :], t1[:, :], ALU.mult))

            def scale(g, s):
                dve.wait_ge(centred, g + 1)
                wait(dve, turned, g - 1)
                dve.tensor_tensor(u[:, s, :, ::-1], dif[:, s, :, :],
                                  rs[:, :].rearrange("p (o t) -> p o t", o=1).to_broadcast([P, CG, L]),
                                  ALU.mult).then_inc(normed, 1)

            def add(g, s):
                dve.wait_ge(conv, g + 1)
                h = Hc[:, bass.ds(CG * g, CG), :]
                dve.tensor_tensor(h, yps[:, s, :, 0:L], h, ALU.add).then_inc(added, 1)

            scale(0, 0)
            scale(1, 1)
            with dve.Fori(0, NCG // 2 - 1) as it:
                for s in range(2):
                    scale(2 * it + s + 2, s)
                    add(2 * it + s, s)
            for s in range(2):
                add(NCG - 2 + s, s)
            dve.wait_ge(added, NCG)

        @block.gpsimd
        def _(pool):
            pool.wait_ge(ln1, 2)

            def centre(g, s):
                wait(pool, normed, g - 1)
                pool.tensor_tensor(dif[:, s, :, :], Hc[:, bass.ds(CG * g, CG), :],
                                   m1[:, :].rearrange("p (o t) -> p o t", o=1).to_broadcast([P, CG, L]),
                                   ALU.subtract).then_inc(centred, 1)

            centre(0, 0)
            centre(1, 1)
            with pool.Fori(1, NCG // 2) as it:
                for s in range(2):
                    centre(2 * it + s, s)

        @block.scalar
        def _(act):
            act.wait_ge(ln1, 7)
            act.activation(t1[:, :], v1[:, :], ACT.Sqrt).then_inc(ln1_sqrt, 1)

            def evacuate(g, s):
                act.wait_ge(turned, g + 1)
                wait(act, conv, g - 1)
                act.activation(uT0[:, s, :], tp0[:, s, :], ACT.Copy).then_inc(evac0, 1)
                act.activation(uT1[:, s, :], tp1[:, s, :], ACT.Copy).then_inc(evac0, 1)

            evacuate(0, 0)
            evacuate(1, 1)
            with act.Fori(1, NCG // 2) as it:
                for s in range(2):
                    evacuate(2 * it + s, s)

        @block.tensor
        def _(pe):
            def turn(g, s):
                pe.wait_ge(normed, g + 1)
                wait(pe, evac0, 2 * (g - 1))
                for c in range(CG):
                    pe.transpose(tp0[:, s, c * P:(c + 1) * P], u[:, s, c, L1:L], ident[:, :])
                    mm = pe.transpose(tp1[:, s, c * P:(c + 1) * P], u[:, s, c, 0:L1], ident[:, :])
                mm.then_inc(turned, 1)

            def convolve(g, s, slot, uses):
                pe.wait_ge(evac0, 2 * g + 2)
                pe.wait_ge(skew_in[slot], 16 * uses)
                wait(pe, added, g - 1)
                for c in range(CG):
                    o = yps[:, s, c, :]
                    t = slice(c * P, (c + 1) * P)
                    pe.matmul(o[:, 0:L], uT0[:, s, t], skew[:, slot, c, :], start=(c % 2 == 0), stop=False,
                              skip_group_check=True)
                    mm = pe.matmul(o[:, P:L], uT1[:, s, t], skew[0:L1, slot, c, P - L1:P], start=False, stop=True,
                                   skip_group_check=True)
                mm.then_inc(conv, 1)

            turn(0, 0)
            turn(1, 1)
            for s in range(SKEW_SLOTS):
                convolve(s, s % 2, s, 1)
                turn(s + 2, s % 2)
            with pe.Fori(1, NCG // SKEW_SLOTS - 1) as it:
                for s in range(SKEW_SLOTS):
                    g = it * SKEW_SLOTS + s
                    convolve(g, s % 2, s, it + 1)
                    turn(g + 2, s % 2)
            for s in range(SKEW_SLOTS):
                g = NCG - SKEW_SLOTS + s
                convolve(g, s % 2, s, NCG // SKEW_SLOTS)
                if g + 2 < NCG:
                    turn(g + 2, s % 2)


GROUPS = tuple((n + TG - 1) // TG for n in WAVES)


def gate_groups(eng, w, group):
    g0, g1 = sum(GROUPS[:w]), sum(GROUPS[:w + 1])

    def tokens(g):
        return 0 if g >= g1 else TG if g < g1 - 1 else WAVES[w] - TG * (GROUPS[w] - 1)

    pairs = (g1 - g0 - 4) // 2
    for g in range(g0, g0 + 2):
        group(g, g % 2, tokens(g), tokens(g + 1))
    with eng.Fori(1, pairs + 1) as it:
        for j in range(2):
            group(2 * it + g0 + j, (g0 + j) % 2, TG, TG)
    for g in range(g0 + 2 + 2 * pairs, g1):
        group(g, g % 2, tokens(g), tokens(g + 1))


def tile_loop(eng, tile):
    for i in range(4):
        tile(i, i, 0, first=i == 0)
    with eng.Fori(1, NT // 4 - 1) as it:
        for r in range(4):
            tile(4 * it + r, r, it)
    for i in range(4 * (NT // 4 - 1), NT):
        tile(i, i % 4, i // 4, last=i == NT - 1)


def waits(eng, constant, *counts):
    counts = [(sem, value if isinstance(value, int) else eng.to_reg(value)) for sem, value in counts]
    eng.wait_ge(*constant)
    for sem, value in counts:
        wait(eng, sem, value)


def wait(eng, sem, value):
    if isinstance(value, int) and value <= 0:
        return
    eng.wait_ge(sem, value)


def stage_c(nc, sem, sb, H, Hflat, ident, w_gate, b_gate, b1c, b2, triu_d, tokno_d, padno_d, tileno_d,
            wsplit, rows, out_rows):
    with ExitStack() as st:
        w1s = sb(st, "w1s", [P, 2, 2 * W1F], F16)
        b1s = sb(st, "b1s", [P, E * NB])
        b2s = sb(st, "b2s", [P, E, D])
        dest = [sb(st, f"dest{w}", [P, n], I32) for w, n in enumerate(WAVES)]
        paddest = [sb(st, f"paddest{w}", [P, 8], I32) for w in range(2)]
        padrow = sb(st, "padrow", [P, ROW])
        experts = sb(st, "experts", [1, NT], I32)

        gate_stack = ExitStack()
        gs = gate_stack
        NW = max(P, *WAVES)
        wg_raw = sb(gs, "wg_raw", [P, PB, 2 * E])
        wg = sb(gs, "wg", [P, PB, 2, 2 * E], F16)
        bg = sb(gs, "bg", [P, E])
        triu = sb(gs, "triu", [P, P])
        ones = sb(gs, "ones", [P, NW])
        padno = sb(gs, "padno", [P, 8])
        padpos = sb(gs, "padpos", [P, 8])
        padt = sb(gs, "padt", [P, 8])
        tileno = sb(gs, "tileno", [1, NT])
        tilee = sb(gs, "tilee", [1, NT])
        tilet = sb(gs, "tilet", [1, NT])
        tokno = sb(gs, "tokno", [P, L], I32)
        bn = sb(gs, "bn2", [P, L, 6])
        v2 = sb(gs, "v2", [P, NW])
        t2 = sb(gs, "t2", [P, NW])
        xn4 = sb(gs, "xn4", [P, 2, TG, D])
        hTh = sb(gs, "hTh", [P, 2, TG // 2 * PB * P], F16)
        hTl = sb(gs, "hTl", [P, 2, TG // 2 * PB * P], F16)
        lg = (xn4[:, :, :, :].rearrange("p s i c -> p (s i c)")[:, 0:(NW + NW % 2) * E]
              .rearrange("p (t e) -> p t e", e=E))
        oh = sb(gs, "oh", [P, E, NW])
        pos = sb(gs, "pos", [P, E, NW])
        mx = sb(gs, "mx", [P, NW])
        cnt = sb(gs, "cnt", [P, 8 * E])
        gate_stack.close()
        w2s = sb(st, "w2s", [P, 2, W2F], F16)

        at = [0]

        def take(shape, dt=F32, parts=P):
            n = math.prod(shape) * (1 if dt != F16 else 2) // (1 if dt != F16 else 4)
            v = Hflat[0:parts, at[0]:at[0] + n]
            at[0] += n
            assert at[0] <= WAVES[0] * ROW
            if dt != F32:
                v = v.bitcast(dt)
            names = "abcd"[:len(shape)]
            return v.rearrange(f"p ({' '.join(names)}) -> p {' '.join(names)}", **dict(zip(names[1:], shape[1:])))

        xt = take([4, 2, ROW])
        xn = take([2, 2, D])
        xT = take([2, 2 * TS], F16)
        xTl = take([2, TS], F16)
        gel = take([NB, TS])
        gh = take([2, NB, TS], F16)
        gl = take([2, NB, TS], F16)
        z = take([2, 2, ROW])
        zi = [take([2]).bitcast(I32) for s in range(2)]

        ps = st.enter_context(nc.psum_tensor("cps", [P, 8, 512], F32))

        cc, w1_in, w2_in, sorted0, sorted1 = (sem(s) for s in ("c_consts", "w1_in", "w2_in", "sorted0", "sorted1"))
        g_bn, g_sqrt, g_norm, g_turn, g_high, g_low, g_logit, g_step, wg_high, wg_low = (
            sem(s) for s in ("g_bn", "g_sqrt", "g_norm", "g_turn", "g_high", "g_low", "g_logit",
                             "g_step", "wg_high", "wg_low"))
        ready = [sem(f"dest_ready{w}") for w in range(2)]
        oh_ready, cnt_ready, stats_ready = sem("oh_ready"), sem("cnt_ready"), sem("stats_ready")
        x_in = [sem(f"x_in{s}") for s in range(4)]
        scattered = [sem(f"scattered{s}") for s in range(2)]
        (xn_ready, xT_turned, xT_high, xT_low, g1_done, gel_done, gh_done, gs_done, y_done, z_done, o_done,
         zi_done) = (
            sem(s) for s in ("xn_ready", "xT_turned", "xT_high", "xT_low", "g1_done", "gel_done", "gh_done",
                             "gs_done", "y_done", "z_done", "o_done", "zi_done"))
        block = st.enter_context(nc.Block())

        def turned_tokens(s):
            return ps[:, 2 * s:2 * s + 2, :].rearrange("p a b -> p (a b)")[:, 0:TG // 2 * PB * P]

        def expert_of(eng, i):
            return eng.value_load(experts[0:1, bass.ds(i, 1)], min_val=0, max_val=E - 1)

        def x_rows(i):
            return rows[bass.ds(TS * i, TS), :].rearrange("(p j) c -> p (j c)", j=2)

        def send(pool, w, n0, n1):
            for n in range(n0, n1):
                t = n - WAVES[w]
                source, place = ((H[:, sum(WAVES[:w]) + n, :], dest[w][:, n:n + 1]) if t < 0 else
                                 (padrow[:, :], paddest[w][:, t:t + 1]))
                pool.indirect_dma_start(out=rows, out_offset=bass.IndirectOffsetOnAxis(ap=place, axis=0),
                                        in_=source, in_offset=None, bounds_check=NT * TS - 1,
                                        oob_is_err=False).then_inc((sorted0, sorted1)[w], 16)

        @block.sync
        def _(sp):
            for dst, src in ((wg_raw[:, :, :], w_gate),
                             (bg[:, :], b_gate.partition_broadcast(P)), (triu[:, :], triu_d),
                             (padno[:, :], padno_d), (tileno[:, :], tileno_d), (tokno[:, :], tokno_d),
                             (b1s[:, :], b1c),
                             (b2s[:, :, :].rearrange("p e c -> p (e c)"),
                              b2.rearrange("e c -> (e c)").partition_broadcast(P))):
                sp.dma_start(dst, src).then_inc(cc, 16)
            for h in range(2):
                sp.dma_start(w1s[:, h, :], wsplit[:, h * WF:h * WF + 2 * W1F]).then_inc(w1_in, 16)
            sp.wait_ge(ready[1], 1)
            for h in range(2):
                sp.dma_start(w2s[:, h, :], wsplit[:, h * WF + 2 * W1F:(h + 1) * WF]).then_inc(w2_in, 16)

            def load(i, s):
                wait(sp, xn_ready, i - 3)
                wait(sp, z_done, i - 3)
                sp.dma_start(xt[:, s, :, :].rearrange("p j c -> p (j c)"), x_rows(i)).then_inc(x_in[s], 16)

            n0 = WAVE_TILES[0]
            sp.wait_ge(sorted0, 16 * 2 * WAVE_TILES[0])
            for i in range(4):
                load(i, i)
            with sp.Fori(1, n0 // 4) as it:
                for s in range(4):
                    load(4 * it + s, s)
            sp.wait_ge(sorted1, 16 * 2 * WAVE_TILES[1])
            with sp.Fori(n0 // 4, NT // 4) as it:
                for s in range(4):
                    load(4 * it + s, s)
            for i in range(NT // 4 * 4, NT):
                load(i, i % 4)

        @block.vector
        def _(dve):
            n = [0]

            def step(ins):
                ins.then_inc(g_step, 1)
                n[0] += 1
                dve.wait_ge(g_step, n[0])

            dve.wait_ge(cc, 16 * 8)
            step(dve.memset(padrow[:, :], 0.0))
            step(dve.tensor_scalar(padrow[:, TOKEN:TOKEN + 1].bitcast(I32), padrow[:, 0:1], float(NOWHERE), None, ALU.add))
            step(dve.memset(ones[:, :], 1.0))
            step(dve.tensor_copy(H[:, :, TOKEN].bitcast(I32), tokno[:, :]))

            dve.wait_ge(wg_high, 1)
            dve.scalar_tensor_tensor(wg[:, :, 1, :], wg_raw[:, :, :], WSCALE, wg[:, :, 0, :], ALU.mult,
                                     ALU.subtract).then_inc(wg_low, 1)

            def stats(t):
                dve.bn_stats(bn[:, bass.ds(t, 1), :].rearrange("p o s -> p (o s)"),
                             H[:, bass.ds(t, 1), 0:D].rearrange("p o c -> p (o c)")).then_inc(g_bn, 1)

            with dve.Fori(0, WAVES[0] // 9) as it:
                for i in range(9):
                    stats(9 * it + i)
            for t in range(WAVES[0] // 9 * 9, WAVES[0]):
                stats(t)

            t0, tile0 = 0, 0
            for w, nw in enumerate(WAVES):
                nt = WAVE_TILES[w]
                dve.wait_ge(g_bn, t0 + nw)
                mean, var = H[:, t0:t0 + nw, STAT0], H[:, t0:t0 + nw, STAT1]
                v, t_, r = v2[:, 0:nw], t2[:, 0:nw], mx[:, 0:nw]
                m_even, s_even, m_odd, s_odd = (bn[:, t0:t0 + nw, c] for c in (1, 2, 4, 5))
                step(dve.tensor_tensor(t_, m_even, m_odd, ALU.subtract))
                step(dve.scalar_tensor_tensor(t_, t_, 0.25 * D, t_, ALU.mult, ALU.mult))
                step(dve.tensor_tensor(v, s_even, s_odd, ALU.add))
                step(dve.tensor_tensor(v, v, t_, ALU.add))
                step(dve.tensor_tensor(mean, m_even, m_odd, ALU.add))
                step(dve.tensor_scalar(mean, mean, 0.5, None, ALU.mult))
                dve.tensor_scalar(v, v, 1.0 / D, EPS, ALU.mult, ALU.add).then_inc(stats_ready, 1)
                dve.wait_ge(g_sqrt, w + 1)
                step(dve.reciprocal(r, t_))
                step(dve.tensor_tensor(t_, r, r, ALU.mult))
                step(dve.tensor_tensor(t_, t_, v, ALU.mult))
                step(dve.tensor_scalar(t_, t_, -0.5, 1.5, ALU.mult, ALU.add))
                step(dve.tensor_tensor(r, r, t_, ALU.mult))
                step(dve.tensor_tensor(t_, mean, r, ALU.mult))
                step(dve.tensor_scalar(var, t_, -1.0, None, ALU.mult))
                dve.tensor_copy(mean, r).then_inc(stats_ready, 1)

                def group(g, s, k, ahead, w=w):
                    dve.wait_ge(g_high, g + 1)
                    wait(dve, g_logit, g - 1)
                    dve.tensor_tensor(hTl[:, s, :], turned_tokens(s), hTh[:, s, :], ALU.subtract).then_inc(g_low, 1)
                    if w == 0:
                        for i in range(AHEAD):
                            stats(AHEAD * g + WAVES[0] + i)

                gate_groups(dve, w, group)
                if w == 0:
                    for t in range(WAVES[0] + AHEAD * GROUPS[0], L):
                        stats(t)

                dve.wait_ge(g_logit, sum(GROUPS[:w + 1]))
                lw, np_ = lg[:, 0:nw, :], (nw + 1) // 2
                parts = (ps[:, 4:6, :].rearrange("p a b -> p (a b)")[:, 0:4 * E * np_]
                         .rearrange("p (t h e) -> p t h e", h=2, e=2 * E))
                lp = lg[:, 0:2 * np_, :].rearrange("p (t s) e -> p t (s e)", s=2)
                step(dve.tensor_copy(lp, parts[:, :, 1, :]))
                step(dve.tensor_tensor(lp, parts[:, :, 0, :], lp, ALU.add))
                step(dve.scalar_tensor_tensor(lw, lw, 1 / WSCALE, bg[:, :].rearrange("p (o e) -> p o e", o=1)
                                              .to_broadcast([P, nw, E]), ALU.mult, ALU.add))
                step(dve.tensor_reduce(mx[:, 0:nw], lw, AX_X, ALU.max))
                step(dve.tensor_tensor(lw, lw, mx[:, 0:nw].rearrange("p (t o) -> p t o", o=1).to_broadcast([P, nw, E]), ALU.is_ge))
                step(dve.tensor_copy(oh[:, 0, 0:nw], lw[:, :, 0]))
                step(dve.tensor_copy(mx[:, 0:nw], lw[:, :, 0]))
                for e in range(1, E - 1):
                    step(dve.tensor_tensor(oh[:, e, 0:nw], lw[:, :, e], mx[:, 0:nw], ALU.is_gt))
                    step(dve.tensor_tensor(mx[:, 0:nw], lw[:, :, e], mx[:, 0:nw], ALU.max))
                dve.tensor_tensor(oh[:, E - 1, 0:nw], lw[:, :, E - 1], mx[:, 0:nw], ALU.is_gt).then_inc(oh_ready, 1)

                dve.wait_ge(cnt_ready, w + 1)
                before = ps[:, 4:6, :].rearrange("p a (b t) -> p (a b) t", b=2)
                column = ps[:, 6:8, :].rearrange("p a (b t) -> p (a b) t", b=2)
                for e in range(E):
                    step(dve.tensor_tensor_scan(pos[:, e, 0:nw], ones[:, 0:nw], column[:, e, 0:nw], 0.0, ALU.mult, ALU.add))
                tot, size, end, base, gap, pad_at = (cnt[:, E * k:E * k + E] for k in range(6))
                step(dve.tensor_copy(tot, pos[:, :, nw - 1]))
                step(dve.tensor_scalar(size, tot, 1.0 / TS, (TS - 1.0) / TS - 0.5 + 0.5 / TS, ALU.mult, ALU.add))
                step(dve.tensor_scalar(size, size, MAGIC, None, ALU.add))
                step(dve.tensor_scalar(size, size, MAGIC, float(TS), ALU.subtract, ALU.mult))
                step(dve.tensor_tensor_scan(end, ones[:, 0:E], size, 0.0, ALU.mult, ALU.add))
                step(dve.tensor_tensor(base, end, size, ALU.subtract))
                step(dve.tensor_tensor(gap, size, tot, ALU.subtract))
                step(dve.tensor_tensor_scan(pad_at, ones[:, 0:E], gap, 0.0, ALU.mult, ALU.add))
                pw = pos[:, :, 0:nw]
                step(dve.tensor_tensor(pw, pw, column[:, :, 0:nw], ALU.subtract))
                step(dve.tensor_tensor(pw, before[:, :, 0:nw], pw, ALU.add))
                step(dve.tensor_tensor(pw, pw, base.rearrange("p (e o) -> p e o", o=1).to_broadcast([P, E, nw]), ALU.add))
                step(dve.tensor_tensor(pw, pw, oh[:, :, 0:nw], ALU.mult))
                step(dve.tensor_reduce(v, pw.rearrange("p e t -> p t e"), AX_X, ALU.add))
                step(dve.tensor_scalar(dest[w][:, :], v, float(TS * tile0), None, ALU.add))
                step(dve.tensor_scalar(padpos[:, :], padno[:, :], tot[:, 0:1], None, ALU.add))
                for e in range(1, E):
                    step(dve.tensor_scalar(padt[:, :], padno[:, :], pad_at[:, e - 1:e], tot[:, e:e + 1], ALU.is_ge, ALU.mult))
                    step(dve.tensor_tensor(padpos[:, :], padpos[:, :], padt[:, :], ALU.add))
                step(dve.tensor_scalar(paddest[w][:, :], padpos[:, :], float(TS * tile0), None, ALU.add))
                te, tt, tn = (a[:, tile0:tile0 + nt] for a in (tilee, tilet, tileno))
                step(dve.tensor_scalar(te, tn, base[0:1, 1:2], None, ALU.is_ge))
                for e in range(2, E):
                    step(dve.tensor_scalar(tt, tn, base[0:1, e:e + 1], None, ALU.is_ge))
                    step(dve.tensor_tensor(te, te, tt, ALU.add))
                dve.tensor_copy(experts[:, tile0:tile0 + nt], te).then_inc(ready[w], 1)
                dve.wait_ge(ready[w], 1)
                t0 += nw
                tile0 += nt

            def split_x(i, s):
                dve.wait_ge(xT_high, i + 1)
                dve.tensor_tensor(xTl[:, s, :], ps[:, 7, 0:TS], xT[:, s, 0:TS], ALU.subtract).then_inc(xT_low, 1)
                dve.tensor_tensor(xT[0:LOW, s, TS:2 * TS], ps[LOW:P, 7, TS:2 * TS], xT[LOW:P, s, TS:2 * TS],
                                  ALU.subtract).then_inc(xT_low, 1)

            def split_h(i, s, b):
                dve.wait_ge(gel_done, NB * i + b + 2)
                wait(dve, y_done, i - 1)
                dve.tensor_copy(gh[:, s, b:b + 2, :], gel[:, b:b + 2, :]).then_inc(gh_done, 1)
                dve.wait_ge(gh_done, NB // 2 * i + b // 2 + 1)
                dve.tensor_tensor(gl[:, s, b:b + 2, :], gel[:, b:b + 2, :], gh[:, s, b:b + 2, :],
                                  ALU.subtract).then_inc(gs_done, 1)

            def output(i, s):
                dve.wait_ge(y_done, i + 1)
                dve.wait_ge(z_done, i + 1)
                dve.scalar_tensor_tensor(z[:, s, :, 0:D], ps[:, 5 + s, :].rearrange("p (j c) -> p j c", j=2)[:, :, 0:D],
                                         1 / WSCALE, z[:, s, :, 0:D], ALU.mult, ALU.add).then_inc(o_done, 1)

            def tile(i, r, it, first=False, last=False):
                split_h(i, r % 2, 0)
                split_h(i, r % 2, 2)
                if not last:
                    split_x(i + 1, (r + 1) % 2)
                split_h(i, r % 2, 4)
                if not first:
                    output(i - 1, (r + 1) % 2)

            split_x(0, 0)
            tile_loop(dve, tile)
            output(NT - 1, (NT - 1) % 2)

        @block.scalar
        def _(act):
            act.wait_ge(cc, 16 * 8)
            act.activation(wg[:, :, 0, :], wg_raw[:, :, :], ACT.Copy, scale=WSCALE).then_inc(wg_high, 1)
            for w, nw in enumerate(WAVES):
                act.wait_ge(stats_ready, 2 * w + 1)
                act.activation(t2[:, 0:nw], v2[:, 0:nw], ACT.Sqrt).then_inc(g_sqrt, 1)
                act.wait_ge(stats_ready, 2 * w + 2)

                def normalise(g, s, k=TG, w=w):
                    wait(act, g_turn, g - 1)
                    tb = TG * (g - sum(GROUPS[:w])) + sum(WAVES[:w])
                    for i in range(k):
                        t = tb + i
                        row = H[:, bass.ds(t, 1), :].rearrange("p o c -> p (o c)")
                        act.activation(xn4[:, s, i, :], row[:, 0:D], ACT.Identity, bias=row[:, STAT1:STAT1 + 1],
                                       scale=row[:, STAT0:STAT0 + 1]).then_inc(g_norm, 1)

                def group(g, s, k, ahead):
                    if ahead:
                        normalise(g + 1, 1 - s, ahead)
                    act.wait_ge(g_turn, g + 1)
                    wait(act, g_logit, g - 1)
                    act.activation(hTh[:, s, :], turned_tokens(s), ACT.Copy).then_inc(g_high, 1)

                g0 = sum(GROUPS[:w])
                normalise(g0, g0 % 2)
                gate_groups(act, w, group)

            def norm_x(i, x_slot, s, uses):
                act.wait_ge(x_in[x_slot], 16 * uses)
                wait(act, xT_turned, i - 1)
                for j in range(2):
                    row = xt[:, x_slot, j, :]
                    a = act.activation(xn[:, s, j, :], row[:, 0:D], ACT.Identity, bias=row[:, STAT1:STAT1 + 1],
                                       scale=row[:, STAT0:STAT0 + 1])
                a.then_inc(xn_ready, 1)

            def high_x(i, s):
                act.wait_ge(xT_turned, i + 1)
                wait(act, g1_done, NB * (i - 1))
                act.activation(xT[:, s, :], ps[:, 7, :], ACT.Copy).then_inc(xT_high, 1)

            def gelu(i, b, r, ex):
                bank = (2 * r + b) % 4
                act.wait_ge(g1_done, NB * i + b + 1)
                wait(act, gs_done, NB // 2 * (i - 1) + b // 2 + 1)
                act.activation(gel[:, b, :], ps[:, bank, 0:TS], ACT.Gelu,
                               bias=b1s[:, bass.ds(NB * ex + b, 1)], scale=1 / WSCALE).then_inc(gel_done, 1)

            def tile(i, r, it, first=False, last=False):
                ex = expert_of(act, i)
                for b in range(NB):
                    gelu(i, b, r, ex)
                    if b == 2 and not last:
                        high_x(i + 1, (r + 1) % 2)
                    if b == 4 and not (isinstance(i, int) and i + 2 >= NT):
                        norm_x(i + 2, (r + 2) % 4, r % 2, it + (r + 2) // 4 + 1)

            act.wait_ge(ready[1], 1)
            norm_x(0, 0, 0, 1)
            norm_x(1, 1, 1, 1)
            high_x(0, 0)
            tile_loop(act, tile)

        @block.tensor
        def _(pe):
            pe.wait_ge(cc, 16 * 8)
            pe.wait_ge(wg_low, 1)
            for w, nw in enumerate(WAVES):
                def turn(g, s, k=TG, w=w):
                    pe.wait_ge(g_norm, TG * (g - sum(GROUPS[:w])) + sum(WAVES[:w]) + k)
                    wait(pe, g_high, g - 1)
                    wait(pe, g_low, g - 1)
                    for i in range((k + 1) // 2 * PB):
                        mm = pe.transpose(turned_tokens(s)[:, i * P:(i + 1) * P],
                                          xn4[:, s, :, :].rearrange("p i c -> p (i c)")[:, i * P:(i + 1) * P], ident[:, :])
                    mm.then_inc(g_turn, 1)

                def logits(g, s, k=TG, w=w):
                    pe.wait_ge(g_low, g + 1)
                    tb = TG * (g - sum(GROUPS[:w]))
                    psl = ps[:, 4:6, :].rearrange("p a b -> p (a b)")
                    for i in range((k + 1) // 2 * PB):
                        blk, n, c = slice(i * P, (i + 1) * P), i % PB, 2 * E * tb + 4 * E * (i // PB)
                        pe.matmul(psl[:, bass.ds(c, 4 * E)], hTh[:, s, blk], wg[:, n, :, :].rearrange("p h e -> p (h e)"),
                                  start=(n == 0), stop=False, skip_group_check=True)
                        mm = pe.matmul(psl[:, bass.ds(c, 2 * E)], hTl[:, s, blk], wg[:, n, 0, :],
                                       start=False, stop=(n == PB - 1), skip_group_check=True)
                    mm.then_inc(g_logit, 1)

                g0 = sum(GROUPS[:w])
                if w:
                    pe.wait_ge(ready[w - 1], 1)
                def group(g, s, k, ahead):
                    if ahead:
                        turn(g + 1, 1 - s, ahead)
                    logits(g, s, k)

                turn(g0, g0 % 2)
                gate_groups(pe, w, group)
                pe.wait_ge(oh_ready, w + 1)
                before = ps[:, 4:6, :].rearrange("p a (b t) -> p (a b) t", b=2)
                column = ps[:, 6:8, :].rearrange("p a (b t) -> p (a b) t", b=2)
                for e in range(E):
                    pe.matmul(before[:, e, 0:nw], triu[:, :], oh[:, e, 0:nw], start=True, stop=True, skip_group_check=True)
                    mm = pe.matmul(column[:, e, 0:nw], ones[:, 0:P], oh[:, e, 0:nw], start=True, stop=True, skip_group_check=True)
                mm.then_inc(cnt_ready, 1)

            pe.wait_ge(ready[1], 1)
            pe.wait_ge(w1_in, 32)

            def turn_x(i, s):
                pe.wait_ge(xn_ready, i + 1)
                wait(pe, xT_high, i)
                wait(pe, xT_low, 2 * i)
                for j in range(2):
                    pe.transpose(ps[:, 7, j * P:(j + 1) * P], xn[:, s, j, 0:P], ident[:, :])
                    mm = pe.transpose(ps[:, 7, TS + j * P:TS + (j + 1) * P], xn[:, s, j, LOW:D], ident[:, :])
                mm.then_inc(xT_turned, 1)

            def layer1(i, b, r, s, ex):
                bank = (2 * r + b) % 4
                if b == 0:
                    pe.wait_ge(xT_low, 2 * i + 2)
                wait(pe, gel_done, NB * i + b - 3)
                o = ps[:, bank, 0:TS]
                for n, (h, part, mov) in enumerate(((0, 0, xT[:, s, 0:TS]), (1, 0, xT[:, s, 0:TS]), (0, 0, xTl[:, s, :]),
                                                    (0, 1, xT[:, s, TS:2 * TS]), (1, 1, xT[:, s, TS:2 * TS]))):
                    mm = pe.matmul(o, w1s[:, h, bass.ds(ex * HID + part * W1F + b * P, P)], mov,
                                   start=(n == 0), stop=(n == 4))
                mm.then_inc(g1_done, 1)

            def layer2(i, b, s, ex):
                if b == 0:
                    wait(pe, o_done, i - 1)
                if b % 2 == 0:
                    pe.wait_ge(gs_done, NB // 2 * i + b // 2 + 1)
                for j in range(2):
                    t = slice(j * P, (j + 1) * P)
                    o = ps[:, 5 + s, j * TS:j * TS + D]
                    for n, (g, h) in enumerate(((gh, 0), (gh, 1), (gl, 0))):
                        mm = pe.matmul(o, g[:, s, b, t], w2s[:, h, bass.ds(ex * (NB * D) + b * D, D)],
                                       start=(b == 0 and j == 0 and n == 0), stop=(b == NB - 1 and n == 2),
                                       skip_group_check=True)
                if b == NB - 1:
                    mm.then_inc(y_done, 1)

            def tile(i, r, it, first=False, last=False):
                ex = expert_of(pe, i)
                prev = None if first else expert_of(pe, i - 1)
                for b in range(NB):
                    layer1(i, b, r, r % 2, ex)
                    if not first:
                        layer2(i - 1, b, (r + 1) % 2, prev)
                    if b == 2 and not last:
                        turn_x(i + 1, (r + 1) % 2)

            turn_x(0, 0)
            pe.wait_ge(w2_in, 32)
            tile_loop(pe, tile)
            prev = expert_of(pe, NT - 1)
            for b in range(NB):
                layer2(NT - 1, b, (NT - 1) % 2, prev)

        @block.gpsimd
        def _(pool):
            pool.wait_ge(ready[0], 1)
            send(pool, 0, 0, 2 * WAVE_TILES[0])

            def residual(i, x_slot, s, uses):
                ex = expert_of(pool, i)
                waits(pool, (ready[1], 1), (x_in[x_slot], 16 * uses), (scattered[s], uses_scatter(i, s)))
                bias = b2s[:, bass.ds(ex, 1), :].to_broadcast([P, 2, D])
                pool.tensor_copy(zi[s], xt[:, x_slot, :, TOKEN].bitcast(I32)).then_inc(zi_done, 1)
                pool.tensor_tensor(z[:, s, :, 0:D], xt[:, x_slot, :, 0:D], bias, ALU.add).then_inc(z_done, 1)

            def uses_scatter(i, s):
                return 32 * (i // 2) if isinstance(i, int) else 16 * (i - s)

            def store(i, s):
                waits(pool, (ready[1], 1), (o_done, i + 1), (zi_done, i + 1))
                for j in range(2):
                    pool.indirect_dma_start(out=out_rows, out_offset=bass.IndirectOffsetOnAxis(ap=zi[s][:, j:j + 1], axis=0),
                                            in_=z[:, s, j, 0:D], in_offset=None, bounds_check=B * L - 1,
                                            oob_is_err=False).then_inc(scattered[s], 16)

            def tile(i, r, it, first=False, last=False):
                residual(i, r, r % 2, it + 1)
                if not first:
                    store(i - 1, (r + 1) % 2)

            for i in range(WAVE_TILES[0]):
                tile(i, i % 4, i // 4, first=i == 0)
                send(pool, 1, *(min(SEND_FIRST + SEND * j, 2 * WAVE_TILES[1]) if j else 0 for j in (i, i + 1)))
            with pool.Fori(WAVE_TILES[0] // 4, NT // 4) as it:
                for r in range(4):
                    tile(4 * it + r, r, it)
            for i in range(NT // 4 * 4, NT):
                tile(i, i % 4, i // 4)
            store(NT - 1, (NT - 1) % 2)
            for s in range(2):
                pool.wait_ge(scattered[s], 32 * ((NT - s + 1) // 2))



def kernel(x, cls_tok, L0_tok_W_proj, L0_tok_b_proj, L0_attn_w1, L0_attn_b1, L0_attn_w2, L0_attn_b2, L0_attn_w3,
           L0_attn_b3, L0_attn_freq, L0_attn_deltas_abs, L0_attn_bias, L0_ffn_Wg, L0_ffn_bg, L0_ffn_W1, L0_ffn_b1,
           L0_ffn_W2, L0_ffn_b2):
    import numpy as np
    import concourse.bacc as bacc
    from concourse.bass_utils import run_bass_kernel_spmd

    def a(v):
        return np.ascontiguousarray(v)

    t = np.linspace(0.0, 1.0, L, dtype=np.float32)
    w = (np.float32(2 * np.pi) * np.linspace(0.0, float(L - 1), L, dtype=np.float32) / np.float32(L)).astype(np.float32)
    fw = np.float32(0.0001) * w
    z = np.stack([t, np.cos(fw), -np.sin(fw)]).astype(np.float32)
    p = np.arange(P)

    wg_pair = np.zeros((2, D, 2, E), np.float32)
    wg_pair[0, :, 0], wg_pair[1, :, 1] = L0_ffn_Wg, L0_ffn_Wg
    wg_pair = a(wg_pair.reshape(PB, P, 2 * E).transpose(1, 0, 2))

    arrays = {
        "x": a(x), "cls_tok": a(cls_tok).reshape(D),
        "wprojT": a(a(L0_tok_W_proj).T), "b_proj": a(L0_tok_b_proj),
        "zT": a(z), "trow": t,
        "fw1T": a(a(L0_attn_w1).T), "fw2T": a(a(L0_attn_w2).T), "fw3T": a(a(L0_attn_w3).T),
        "fcols": a(np.stack([a(L0_attn_b1), a(L0_attn_b2), a(L0_attn_freq), a(L0_attn_freq)], axis=1)),
        "f3cols": a(np.concatenate([a(v).reshape(2, 96).T for v in (L0_attn_b3, L0_attn_deltas_abs, L0_attn_bias)], axis=1)),
        "w_gate": wg_pair, "b_gate": a(L0_ffn_bg),
        "w1": a(L0_ffn_W1), "b1c": a(a(L0_ffn_b1).reshape(E * NB, P).T),
        "w2": a(L0_ffn_W2), "b2": a(L0_ffn_b2),
        "ident_d": np.eye(P, dtype=np.float32),
        "triu_d": np.triu(np.ones((P, P), np.float32), 1),
        "tokno_d": a((p[:, None] * L + np.arange(L)[None]).astype(np.int32)),
        "padno_d": a((np.arange(8)[None] * P + p[:, None]).astype(np.float32)),
        "tileno_d": np.concatenate([np.arange(n) * TS for n in WAVE_TILES]).astype(np.float32)[None],
    }
    nc = bacc.Bacc("TRN2", target_bir_lowering=False, num_devices=1)
    args = {n: nc.dram_tensor(n, v.shape, mybir.dt.from_np(v.dtype), kind="ExternalInput").ap() for n, v in arrays.items()}
    out = nc.dram_tensor("out", (B, L, D), F32, kind="ExternalOutput").ap()
    vit_block(nc, **args, out=out)
    return run_bass_kernel_spmd(nc, [arrays], core_ids=[0]).results[0]["out"]
```

```python
from contextlib import ExitStack
import math

import concourse.bass as bass
from concourse import mybir

P = 128
F32 = mybir.dt.float32
F16 = mybir.dt.float16
I32 = mybir.dt.int32
ALU = mybir.AluOpType
ACT = mybir.ActivationFunctionType
AX_X = mybir.AxisListType.X

B, IC, IMG = 128, 3, 224
PS = 16
G = IMG // PS
L = 1 + G * G
D = 192
E = 4
HID = 768
FO = 16
EPS = 1e-5

KC = IC * PS * PS // P
ROWS = 8
CHUNK = ROWS * IMG
HALF = G // 2
HT = HALF * P

CG = 4
NCG = D // CG
L1 = L - P
PADDED = P - 1 + L
SKEW_SLOTS = 4

ROW = 196
STAT0, STAT1, TOKEN = 192, 193, 194

TS = 256
NB = HID // P
WAVES = (74, 123)
TG = 4
PB = 2 * D // P
BY_ACT = (3, 2)
AHEAD = 5
WSCALE = 64.0
LOW = 64
NOWHERE = 1 << 20
MAGIC = 1.5 * 2.0 ** 23
WAVE_TILES = tuple((n * P + E * (TS - 1)) // TS for n in WAVES)
NT = sum(WAVE_TILES)
W1F = E * HID
W2F = E * NB * D
WF = 2 * W1F + W2F
SEND_FIRST = 8
assert sum(WAVES) == L and WAVE_TILES[0] % 4 == 0 and TG % 2 == 0 and E * max(WAVES) <= 512


def vit_block(nc, x, cls_tok, wprojT, b_proj, zT, trow, fw1T, fw2T, fw3T, fcols, f3cols,
              w_gate, b_gate, w1, b1c, w2, b2, ident_d, triu_d, tokno_d, padno_d, tileno_d, out):
    kpad = nc.dram_tensor("kpad", (D, PADDED), F32).ap()
    wsplit = nc.dram_tensor("wsplit", (P, 2 * WF), F16).ap()
    rows = nc.dram_tensor("rows", (NT * TS, ROW), F32).ap()
    out_rows = out.rearrange("b t c -> (b t) c")
    x_chunks = x.rearrange("b c (r y) w -> b c r (y w)", y=ROWS)

    with ExitStack() as whole:
        def sem(name):
            return whole.enter_context(nc.semaphore(name))

        def sb(stack, name, shape, dt=F32):
            return stack.enter_context(nc.sbuf_tensor(name, shape, dt))

        H = sb(whole, "H", [P, L, ROW])
        ident = sb(whole, "ident", [P, P])
        Hflat = H[:, :, :].rearrange("p t c -> p (t c)")

        stage_a(nc, sem, sb, H, Hflat, ident, x_chunks, cls_tok, wprojT, b_proj, zT, trow, fw1T, fw2T,
                fw3T, fcols, f3cols, w1, w2, ident_d, kpad, wsplit)
        stage_b(nc, sem, sb, H, ident, kpad)
        stage_c(nc, sem, sb, H, Hflat, ident, w_gate, b_gate, b1c, b2, triu_d, tokno_d, padno_d, tileno_d,
                wsplit, rows, out_rows)


def stage_a(nc, sem, sb, H, Hflat, ident, x_chunks, cls_tok, wprojT, b_proj, zT, trow, fw1T, fw2T, fw3T,
            fcols, f3cols, w1, w2, ident_d, kpad, wsplit):
    with ExitStack() as st:
        xr = sb(st, "xr", [P, KC, CHUNK])
        xh = sb(st, "xh", [P, 2, HT], F16)
        xl = sb(st, "xl", [P, 2, HT], F16)
        wp = sb(st, "wp", [P, 2, KC, D], F16)
        bp = sb(st, "bp", [P, D])
        bn = sb(st, "bn", [P, HALF, 6])
        tp = [st.enter_context(nc.psum_tensor(f"tp{i}", [P, 1024], F32)) for i in range(2)]
        acc = st.enter_context(nc.psum_tensor("acc", [P, 8, 256], F32))

        tail = (L - HALF) * ROW
        base = tail - 2 * WF
        w_raw = Hflat[:, base:base + WF]
        w_hl = Hflat[:, base + WF:base + 2 * WF].bitcast(F16).rearrange("p (h f) -> p h f", h=2)
        at = [48 * ROW]
        SPLIT_ROWS = (1, 3)
        PIECES = 2 * KC * (SPLIT_ROWS[1] - SPLIT_ROWS[0])
        PIECE = WF // PIECES
        assert WF % PIECES == 0 and base > (1 + 5 * G) * ROW and at[0] > (1 + 3 * G) * ROW

        def stage(parts, n):
            v = Hflat[0:parts, at[0]:at[0] + n]
            at[0] += n
            return v

        wp_raw = stage(P, KC * D).rearrange("p (k e) -> p k e", k=KC)
        xp_b = sb(st, "xp_b", [P, 4 * P])
        xp = ((Hflat[:, tail:tail + 4 * P], Hflat[:, tail + 4 * P:tail + 7 * P]),
              (xp_b[:, :], Hflat[:, tail + 7 * P:tail + 10 * P]))
        z_s, t_s = stage(3, L), stage(96, L)
        fw1_s, fw2_s, fw3_s = stage(3, FO), stage(FO, FO), stage(FO, D)
        fc = stage(FO, 4)
        f3 = stage(96, 8)
        ang, nr, nf, hid = stage(FO, L), stage(FO, L), stage(FO, L), stage(FO, L)
        decay = stage(96, 2 * L).rearrange("p (h t) -> p h t", h=2)
        kp = stage(96, 2 * PADDED).rearrange("p (h t) -> p h t", h=2)

        OUT = ((0, 2), (2, 4), (4, HALF))
        consts_in, proj_in, wraw_in, cls_in, kpad_out, wsplit_out = (
            sem(s) for s in ("consts_in", "proj_in", "wraw_in", "cls_in", "kpad_out", "wsplit_out"))
        chunk_in = [sem(f"chunk_in{k}") for k in range(KC)]
        f_mm, f_dve, f_act, wsp_hi, wsp_lo = (sem(s) for s in ("f_mm", "f_dve", "f_act", "wsp_hi", "wsp_lo"))
        turned, high, low, half_acc, bn_done, stats_done = (
            sem(s) for s in ("turned", "high", "low", "half_acc", "bn_done", "stats_done"))
        half_out = [sem(f"half_out{c}") for c in range(len(OUT))]
        ordered = [sem(f"ordered{c}") for c in range(2)]

        block = st.enter_context(nc.Block())

        def patches(n, c):
            g0, g1 = n // KC * HALF + 4 * c, n // KC * HALF + (4, HALF)[c]
            return (xp[n % 2][c].rearrange("p (g y w) -> p g y w", y=ROWS, w=PS),
                    xr[:, n % KC, :].rearrange("p (y g w) -> p g y w", y=ROWS, w=PS)[:, g0:g1, :, :])

        @block.sync
        def _(sp):
            for k in range(KC):
                if k == 0:
                    sp.wait_ge(consts_in, 16 * 7)
                sp.dma_start(xr[:, k, :], x_chunks[:, k // 2, k % 2, :]).then_inc(chunk_in[k], 16)
                if k == 0:
                    sp.dma_start(ident[:, :], ident_d).then_inc(proj_in, 16)
                    sp.dma_start(wp_raw, wprojT.rearrange("(k p) e -> p k e", p=P)).then_inc(proj_in, 16)
                    sp.dma_start(bp[:, :], b_proj.partition_broadcast(P)).then_inc(proj_in, 16)
            with sp.Fori(1, G) as gy:
                for k in range(KC):
                    for c in range(2):
                        sp.wait_ge(ordered[c], 2 * KC * gy - KC + k + 1)
                    sp.dma_start(xr[:, k, :], x_chunks[:, k // 2, bass.ds(2 * gy + k % 2, 1), :]
                                 .rearrange("b o w -> b (o w)")).then_inc(chunk_in[k], 16)
            sp.wait_ge(kpad_out, 16)
            sp.wait_ge(wsplit_out, 16)

        @block.scalar
        def _(act):
            for dst, src in ((fw1_s, fw1T), (z_s, zT), (fc, fcols), (fw2_s, fw2T), (fw3_s, fw3T),
                             (t_s, trow.partition_broadcast(96)), (f3[:, 0:6], f3cols)):
                act.dma_start(dst, src).then_inc(consts_in, 16)
            act.dma_start(H[:, 0, 0:D], cls_tok.partition_broadcast(P)).then_inc(cls_in, 16)
            act.wait_ge(consts_in, 16 * 7)
            for n in range(2):
                act.wait_ge(f_dve, 7 * n + 8)
                act.activation(hid, ang, ACT.Sin).then_inc(f_act, 1)
            act.wait_ge(f_dve, 16)
            for h in range(2):
                act.activation(decay[:, h, :], t_s, ACT.Exp, scale=f3[:, 6 + h:7 + h]).then_inc(f_act, 1)
            act.wait_ge(proj_in, 16 * 3)
            act.activation(wp[:, 0, :, :], wp_raw, ACT.Copy, scale=WSCALE).then_inc(wsp_hi, 1)
            act.dma_start(w_raw[:, 0:W1F].rearrange("p (e h) -> p e h", e=E),
                          w1[:, 0:P, :].rearrange("e c h -> c e h")).then_inc(wraw_in, 16)
            for s in range(2):
                act.dma_start(w_raw[s * LOW:(s + 1) * LOW, W1F:2 * W1F].rearrange("p (e h) -> p e h", e=E),
                              w1[:, P:D, :].rearrange("e c h -> c e h")).then_inc(wraw_in, 16)
            act.dma_start(w_raw[:, 2 * W1F:WF].rearrange("p (k c) -> p k c", c=D),
                          w2.rearrange("e (k p) c -> p (e k) c", p=P)).then_inc(wraw_in, 16)
            def split_high(piece):
                v = bass.ds(piece * PIECE, PIECE)
                act.activation(w_hl[:, 0, v], w_raw[:, v], ACT.Copy, scale=WSCALE).then_inc(wsp_hi, 1)

            def high_part(n, q):
                act.wait_ge(turned, q + 1)
                wait(act, half_acc, len(OUT) * (q - 1))
                act.activation(xh[:, n % 2, :], tp[n % 2][:, 0:HT], ACT.Copy).then_inc(high, 1)

            def order(n, gy, q):
                act.wait_ge(chunk_in[n % KC], 16 * (gy + 1))
                wait(act, turned, q - 1)
                dst, src = patches(n, 0)
                act.activation(dst, src, ACT.Copy).then_inc(ordered[0], 1)

            order(0, 0, 0)
            order(1, 0, 1)
            for n in range(2 * KC):
                high_part(n, n)
                order((n + 2) % (2 * KC), (n + 2) // (2 * KC), n + 2)
            act.wait_ge(wraw_in, 64)
            for g0, g1 in (SPLIT_ROWS, (SPLIT_ROWS[1], G - 1)):
                with act.Fori(g0, g1) as gy:
                    for n in range(2 * KC):
                        high_part(n, 2 * KC * gy + n)
                        order((n + 2) % (2 * KC), gy + (n + 2) // (2 * KC), 2 * KC * gy + n + 2)
                        if (g0, g1) == SPLIT_ROWS:
                            split_high(2 * KC * (gy - g0) + n)
                if (g0, g1) == SPLIT_ROWS:
                    act.wait_ge(wsp_lo, PIECES + 1)
                    act.dma_start(wsplit, w_hl.rearrange("p h f -> p (h f)")).then_inc(wsplit_out, 16)
            for n in range(2 * KC):
                high_part(n, 2 * KC * (G - 1) + n)
                if n + 2 < 2 * KC:
                    order(n + 2, G - 1, 2 * KC * (G - 1) + n + 2)

        @block.tensor
        def _(pe):
            pe.wait_ge(consts_in, 16 * 7)
            pe.matmul(tp[0][0:FO, 0:L], fw1_s, z_s, start=True, stop=True).then_inc(f_mm, 1)
            pe.wait_ge(f_act, 1)
            pe.matmul(tp[1][0:FO, 0:L], fw2_s, hid, start=True, stop=True).then_inc(f_mm, 1)
            pe.wait_ge(f_act, 2)
            for h in range(2):
                pe.matmul(tp[0][0:96, 512 * h:512 * h + L], fw3_s[:, 96 * h:96 * h + 96], hid,
                          start=True, stop=True).then_inc(f_mm, 1)
            pe.wait_ge(f_dve, 18)
            pe.wait_ge(proj_in, 16 * 3)
            pe.wait_ge(wsp_lo, 1)

            def turn(n, q):
                for c in range(2):
                    pe.wait_ge(ordered[c], q + 1)
                wait(pe, low, q - 1)
                for i in range(HALF):
                    piece = xp[n % 2][i // 4]
                    mm = pe.transpose(tp[n % 2][:, i * P:(i + 1) * P], piece[:, i % 4 * P:i % 4 * P + P], ident[:, :])
                mm.then_inc(turned, 1)

            def project(n, q, hn):
                k, s = n % KC, n % 2
                pe.wait_ge(low, q + 1)
                for i in range(HALF):
                    for c, (i0, _) in enumerate(OUT):
                        if k == 0 and i == i0:
                            pe.wait_ge(half_out[c], hn)
                    t = slice(i * P, (i + 1) * P)
                    o = acc[:, i, 0:D]
                    pe.matmul(o, xh[:, s, t], wp[:, 0, k, :], start=(k == 0 and i % 2 == 0), stop=False,
                              skip_group_check=True)
                    pe.matmul(o, xh[:, s, t], wp[:, 1, k, :], start=False, stop=False, skip_group_check=True)
                    mm = pe.matmul(o, xl[:, s, t], wp[:, 0, k, :], start=False, stop=(k == KC - 1),
                                   skip_group_check=True)
                    if i + 1 in [i1 for _, i1 in OUT]:
                        mm.then_inc(half_acc, 1)

            turn(0, 0)
            with pe.Fori(0, G - 1) as gy:
                for n in range(2 * KC):
                    q = 2 * KC * gy + n
                    if n + 1 < 2 * KC:
                        turn(n + 1, q + 1)
                    else:
                        turn(0, q + 1)
                    project(n, q, 2 * gy + n // KC)
            gy = G - 1
            for n in range(2 * KC):
                q = 2 * KC * gy + n
                if n + 1 < 2 * KC:
                    turn(n + 1, q + 1)
                project(n, q, 2 * gy + n // KC)

        @block.vector
        def _(dve):
            nd = [0]

            def f_step(ins):
                ins.then_inc(f_dve, 1)
                nd[0] += 1
                dve.wait_ge(f_dve, nd[0])

            f_step(dve.memset(kp, 0.0))
            dve.wait_ge(consts_in, 16 * 7)
            for n in range(2):
                dve.wait_ge(f_mm, n + 1)
                f_step(dve.tensor_scalar(ang, tp[n][0:FO, 0:L], fc[:, n:n + 1], fc[:, 2:3], ALU.add, ALU.mult))
                f_step(dve.tensor_scalar(nr, ang, 1 / (2 * math.pi), MAGIC, ALU.mult, ALU.add))
                f_step(dve.tensor_scalar(nf, nr, MAGIC, None, ALU.subtract))
                rest = 2 * math.pi
                for bits in (7, 17, 30):
                    part = round(rest * 2 ** bits) / 2 ** bits
                    rest -= part
                    f_step(dve.scalar_tensor_tensor(ang, nf, -part, ang, ALU.mult, ALU.add))
                f_step(dve.tensor_scalar(ang, ang, 3.1415925, -3.1415925, ALU.min, ALU.max))
            f_step(dve.tensor_scalar(f3[:, 6:8], f3[:, 2:4], -1.0, None, ALU.mult))
            for h in range(2):
                dve.wait_ge(f_mm, 3 + h)
                dve.wait_ge(f_act, 3 + h)
                dve.scalar_tensor_tensor(kp[:, h, P - 1:PADDED], tp[0][0:96, 512 * h:512 * h + L], f3[:, h:h + 1],
                                         decay[:, h, :], ALU.add, ALU.mult).then_inc(f_dve, 1)
                nd[0] += 1
            dve.wait_ge(f_dve, nd[0])
            f_step(dve.tensor_scalar(kp[:, :, P - 1:PADDED], kp[:, :, P - 1:PADDED], 1.0 / (2 * L), None, ALU.mult))
            f_step(dve.tensor_tensor(kp[:, :, P - 1], kp[:, :, P - 1], f3[:, 4:6], ALU.add))
            dve.wait_ge(wsp_hi, 1)
            dve.scalar_tensor_tensor(wp[:, 1, :, :], wp_raw, WSCALE, wp[:, 0, :, :], ALU.mult,
                                     ALU.subtract).then_inc(wsp_lo, 1)

            def split_low(piece):
                dve.wait_ge(wsp_hi, piece + 2)
                v = bass.ds(piece * PIECE, PIECE)
                dve.scalar_tensor_tensor(w_hl[:, 1, v], w_raw[:, v], WSCALE, w_hl[:, 0, v], ALU.mult,
                                         ALU.subtract).then_inc(wsp_lo, 1)

            def pairs(v):
                return v.rearrange("p t (h s) -> p t h s", h=2)[:, :, :, 1:3]

            dve.wait_ge(cls_in, 16)
            dve.bn_stats(bn[:, 0, :], H[:, 0, 0:D]).then_inc(bn_done, 1)
            dve.wait_ge(bn_done, 1)
            dve.tensor_copy(H[:, 0:1, D:D + 4], pairs(bn[:, 0:1, :])).then_inc(stats_done, 1)
            dve.wait_ge(stats_done, 1)

            def low_part(n, q):
                dve.wait_ge(high, q + 1)
                dve.tensor_tensor(xl[:, n % 2, :], tp[n % 2][:, 0:HT], xh[:, n % 2, :], ALU.subtract).then_inc(low, 1)

            def tokens_out(hn, t0, parts):
                for c in parts:
                    i0, i1 = OUT[c]
                    dve.wait_ge(half_acc, len(OUT) * (KC * (hn + 1) - 1) + c + 1)
                    dve.scalar_tensor_tensor(
                        H[:, bass.ds(t0 + i0, i1 - i0), 0:D], acc[:, i0:i1, 0:D], 1 / WSCALE,
                        bp[:, :].rearrange("p (o e) -> p o e", o=1).to_broadcast([P, i1 - i0, D]),
                        ALU.mult, ALU.add).then_inc(half_out[c], 1)

            def statistics(hn, i0, i1):
                waits(dve, (cls_in, 16), *((done, hn + 1) for done in half_out),
                      (stats_done, (len(SHARE) - 1) * hn + SHARE.index(i0) + 1))
                for i in range(i0, i1):
                    dve.bn_stats(bn[:, i, :], H[:, bass.ds(1 + HALF * hn + i, 1), 0:D].rearrange("p o c -> p (o c)")
                                 ).then_inc(bn_done, 1)
                dve.wait_ge(bn_done, HALF * hn + i1 + 1)
                dve.tensor_copy(H[:, bass.ds(1 + HALF * hn + i0, i1 - i0), D:D + 4], pairs(bn[:, i0:i1, :])
                                ).then_inc(stats_done, 1)

            SHARE = (0, 2, 3, 5, 6, 7)

            def half_steps(half, hn, first=False, last=False, piece=None):
                q0 = KC * hn
                for k in range(1, KC):
                    if piece is not None:
                        split_low(piece + k - 1)
                    low_part(half * KC + k, q0 + k)
                    if not first:
                        statistics(hn - 1, SHARE[k - 1], SHARE[k])
                tokens_out(hn, 1 + HALF * hn, (0,))
                if not last:
                    if piece is not None:
                        split_low(piece + KC - 1)
                    low_part(half * KC + KC, q0 + KC)
                tokens_out(hn, 1 + HALF * hn, (1, 2))

            low_part(0, 0)
            half_steps(0, 0, first=True)
            half_steps(1, 1)
            for g0, g1 in (SPLIT_ROWS, (SPLIT_ROWS[1], 5), (5, G - 1)):
                if g0 == 3:
                    dve.wait_ge(kpad_out, 16)
                if g0 == 5:
                    dve.wait_ge(wsplit_out, 16)
                with dve.Fori(g0, g1) as gy:
                    for half in range(2):
                        half_steps(half, 2 * gy + half,
                                   piece=2 * KC * (gy - g0) + KC * half if (g0, g1) == SPLIT_ROWS else None)
            for half in range(2):
                half_steps(half, 2 * (G - 1) + half, last=half == 1)
            statistics(2 * G - 1, 0, HALF)
            dve.wait_ge(stats_done, (2 * G - 1) * (len(SHARE) - 1) + 2)

        @block.gpsimd
        def _(pool):
            def order(n, gy, q):
                waits(pool, (consts_in, 16 * 7), (chunk_in[n % KC], 16 * (gy + 1)), (turned, q - 1))
                dst, src = patches(n, 1)
                pool.tensor_copy(dst, src).then_inc(ordered[1], 1)

            order(0, 0, 0)
            order(1, 0, 1)
            pool.wait_ge(f_dve, 20)
            pool.dma_start(kpad.rearrange("(h p) l -> p h l", h=2), kp).then_inc(kpad_out, 16)
            for n in range(2, 2 * KC):
                order(n, 0, n)
            with pool.Fori(1, G) as gy:
                for n in range(2 * KC):
                    order(n, gy, 2 * KC * gy + n)
            pool.wait_ge(kpad_out, 16)


def stage_b(nc, sem, sb, H, ident, kpad):
    with ExitStack() as st:
        m1 = sb(st, "m1", [P, L])
        v1 = sb(st, "v1", [P, L])
        rs = sb(st, "rs", [P, L])
        t1 = sb(st, "t1", [P, L])
        dif = sb(st, "dif", [P, 2, CG, L])
        u = sb(st, "u", [P, 2, CG, L])
        uT0 = sb(st, "uT0", [P, 2, CG * P])
        uT1 = sb(st, "uT1", [L1, 2, CG * P])
        skew = sb(st, "skew", [P, SKEW_SLOTS, CG, L])
        tp0 = st.enter_context(nc.psum_tensor("tp0b", [P, 2, 512], F32))
        tp1 = st.enter_context(nc.psum_tensor("tp1b", [L1, 2, 512], F32))
        yps = st.enter_context(nc.psum_tensor("yps", [P, 2, CG, 256], F32))
        skew_in = [sem(f"skew_in{i}") for i in range(SKEW_SLOTS)]
        ln1, ln1_sqrt, centred, normed, turned, evac0, conv, added = (
            sem(s) for s in ("ln1", "ln1_sqrt", "b_centred", "b_normed", "b_turned", "b_evac", "b_conv", "b_added"))
        Hc = H[:, :, :].rearrange("p t c -> p c t")
        block = st.enter_context(nc.Block())

        def skew_dma(sp, g, s):
            src = kpad[bass.ds(CG * g, CG), 0:L]
            src = bass.AP(src.tensor, src.offset, [[1, P], [PADDED, CG], [1, L]])
            sp.dma_start(skew[:, s, :, :], src).then_inc(skew_in[s], 16)

        @block.sync
        def _(sp):
            for s in range(SKEW_SLOTS):
                skew_dma(sp, s, s)
            with sp.Fori(1, NCG // SKEW_SLOTS) as it:
                for s in range(SKEW_SLOTS):
                    g = it * SKEW_SLOTS + s
                    sp.wait_ge(conv, g - SKEW_SLOTS + 1)
                    skew_dma(sp, g, s)

        @block.vector
        def _(dve):
            n = [0]

            def step(ins):
                ins.then_inc(ln1, 1)
                n[0] += 1
                dve.wait_ge(ln1, n[0])

            m_even, s_even, m_odd, s_odd = (H[:, :, D + c] for c in range(4))
            step(dve.tensor_tensor(m1[:, :], m_even, m_odd, ALU.add))
            step(dve.tensor_scalar(m1[:, :], m1[:, :], 0.5, None, ALU.mult))
            step(dve.tensor_tensor(t1[:, :], m_even, m_odd, ALU.subtract))
            step(dve.scalar_tensor_tensor(t1[:, :], t1[:, :], 0.25 * D, t1[:, :], ALU.mult, ALU.mult))
            step(dve.tensor_tensor(v1[:, :], s_even, s_odd, ALU.add))
            step(dve.tensor_tensor(v1[:, :], v1[:, :], t1[:, :], ALU.add))
            step(dve.tensor_scalar(v1[:, :], v1[:, :], 1.0 / D, EPS, ALU.mult, ALU.add))
            dve.wait_ge(ln1_sqrt, 1)
            step(dve.reciprocal(rs[:, :], t1[:, :]))
            step(dve.tensor_tensor(t1[:, :], rs[:, :], rs[:, :], ALU.mult))
            step(dve.tensor_tensor(t1[:, :], t1[:, :], v1[:, :], ALU.mult))
            step(dve.tensor_scalar(t1[:, :], t1[:, :], -0.5, 1.5, ALU.mult, ALU.add))
            step(dve.tensor_tensor(rs[:, :], rs[:, :], t1[:, :], ALU.mult))

            def scale(g, s):
                dve.wait_ge(centred, g + 1)
                wait(dve, turned, g - 1)
                dve.tensor_tensor(u[:, s, :, ::-1], dif[:, s, :, :],
                                  rs[:, :].rearrange("p (o t) -> p o t", o=1).to_broadcast([P, CG, L]),
                                  ALU.mult).then_inc(normed, 1)

            def add(g, s):
                dve.wait_ge(conv, g + 1)
                h = Hc[:, bass.ds(CG * g, CG), :]
                dve.tensor_tensor(h, yps[:, s, :, 0:L], h, ALU.add).then_inc(added, 1)

            scale(0, 0)
            scale(1, 1)
            with dve.Fori(0, NCG // 2 - 1) as it:
                for s in range(2):
                    scale(2 * it + s + 2, s)
                    add(2 * it + s, s)
            for s in range(2):
                add(NCG - 2 + s, s)
            dve.wait_ge(added, NCG)

        @block.gpsimd
        def _(pool):
            pool.wait_ge(ln1, 2)

            def centre(g, s):
                wait(pool, normed, g - 1)
                pool.tensor_tensor(dif[:, s, :, :], Hc[:, bass.ds(CG * g, CG), :],
                                   m1[:, :].rearrange("p (o t) -> p o t", o=1).to_broadcast([P, CG, L]),
                                   ALU.subtract).then_inc(centred, 1)

            centre(0, 0)
            centre(1, 1)
            with pool.Fori(1, NCG // 2) as it:
                for s in range(2):
                    centre(2 * it + s, s)

        @block.scalar
        def _(act):
            act.wait_ge(ln1, 7)
            act.activation(t1[:, :], v1[:, :], ACT.Sqrt).then_inc(ln1_sqrt, 1)

            def evacuate(g, s):
                act.wait_ge(turned, g + 1)
                wait(act, conv, g - 1)
                act.activation(uT0[:, s, :], tp0[:, s, :], ACT.Copy).then_inc(evac0, 1)
                act.activation(uT1[:, s, :], tp1[:, s, :], ACT.Copy).then_inc(evac0, 1)

            evacuate(0, 0)
            evacuate(1, 1)
            with act.Fori(1, NCG // 2) as it:
                for s in range(2):
                    evacuate(2 * it + s, s)

        @block.tensor
        def _(pe):
            def turn(g, s):
                pe.wait_ge(normed, g + 1)
                wait(pe, evac0, 2 * (g - 1))
                for c in range(CG):
                    pe.transpose(tp0[:, s, c * P:(c + 1) * P], u[:, s, c, L1:L], ident[:, :])
                    mm = pe.transpose(tp1[:, s, c * P:(c + 1) * P], u[:, s, c, 0:L1], ident[:, :])
                mm.then_inc(turned, 1)

            def convolve(g, s, slot, uses):
                pe.wait_ge(evac0, 2 * g + 2)
                pe.wait_ge(skew_in[slot], 16 * uses)
                wait(pe, added, g - 1)
                for c in range(CG):
                    o = yps[:, s, c, :]
                    t = slice(c * P, (c + 1) * P)
                    pe.matmul(o[:, 0:L], uT0[:, s, t], skew[:, slot, c, :], start=(c % 2 == 0), stop=False,
                              skip_group_check=True)
                    mm = pe.matmul(o[:, P:L], uT1[:, s, t], skew[0:L1, slot, c, P - L1:P], start=False, stop=True,
                                   skip_group_check=True)
                mm.then_inc(conv, 1)

            turn(0, 0)
            turn(1, 1)
            for s in range(SKEW_SLOTS):
                convolve(s, s % 2, s, 1)
                turn(s + 2, s % 2)
            with pe.Fori(1, NCG // SKEW_SLOTS - 1) as it:
                for s in range(SKEW_SLOTS):
                    g = it * SKEW_SLOTS + s
                    convolve(g, s % 2, s, it + 1)
                    turn(g + 2, s % 2)
            for s in range(SKEW_SLOTS):
                g = NCG - SKEW_SLOTS + s
                convolve(g, s % 2, s, NCG // SKEW_SLOTS)
                if g + 2 < NCG:
                    turn(g + 2, s % 2)


GROUPS = tuple((n + TG - 1) // TG for n in WAVES)


def gate_groups(eng, w, group):
    g0, g1 = sum(GROUPS[:w]), sum(GROUPS[:w + 1])

    def tokens(g):
        return 0 if g >= g1 else TG if g < g1 - 1 else WAVES[w] - TG * (GROUPS[w] - 1)

    pairs = (g1 - g0 - 4) // 2
    for g in range(g0, g0 + 2):
        group(g, g % 2, tokens(g), tokens(g + 1))
    with eng.Fori(1, pairs + 1) as it:
        for j in range(2):
            group(2 * it + g0 + j, (g0 + j) % 2, TG, TG)
    for g in range(g0 + 2 + 2 * pairs, g1):
        group(g, g % 2, tokens(g), tokens(g + 1))


def tile_loop(eng, tile):
    for i in range(4):
        tile(i, i, 0, first=i == 0)
    with eng.Fori(1, NT // 4 - 1) as it:
        for r in range(4):
            tile(4 * it + r, r, it)
    for i in range(4 * (NT // 4 - 1), NT):
        tile(i, i % 4, i // 4, last=i == NT - 1)


def waits(eng, constant, *counts):
    counts = [(sem, value if isinstance(value, int) else eng.to_reg(value)) for sem, value in counts]
    eng.wait_ge(*constant)
    for sem, value in counts:
        wait(eng, sem, value)


def wait(eng, sem, value):
    if isinstance(value, int) and value <= 0:
        return
    eng.wait_ge(sem, value)


def stage_c(nc, sem, sb, H, Hflat, ident, w_gate, b_gate, b1c, b2, triu_d, tokno_d, padno_d, tileno_d,
            wsplit, rows, out_rows):
    with ExitStack() as st:
        w1s = sb(st, "w1s", [P, 2, 2 * W1F], F16)
        b1s = sb(st, "b1s", [P, E * NB])
        b2s = sb(st, "b2s", [P, E, D])
        dest = [sb(st, f"dest{w}", [P, n], I32) for w, n in enumerate(WAVES)]
        paddest = [sb(st, f"paddest{w}", [P, 8], I32) for w in range(2)]
        padrow = sb(st, "padrow", [P, ROW])
        experts = sb(st, "experts", [1, NT], I32)

        gate_stack = ExitStack()
        gs = gate_stack
        NW = max(P, *WAVES)
        wg_raw = sb(gs, "wg_raw", [P, PB, 2 * E])
        wg = sb(gs, "wg", [P, PB, 2, 2 * E], F16)
        bg2 = sb(gs, "bg2", [P, 2 * E])
        triu_raw = sb(gs, "triu_raw", [P, P])
        triu = sb(gs, "triu", [P, P], F16)
        ones16 = sb(gs, "ones16", [P, P], F16)
        ones = sb(gs, "ones", [P, NW])
        padno = sb(gs, "padno", [P, 8])
        padpos = sb(gs, "padpos", [P, 8])
        padt = sb(gs, "padt", [P, 8])
        tileno = sb(gs, "tileno", [1, NT])
        tilee = sb(gs, "tilee", [1, NT])
        tilet = sb(gs, "tilet", [1, NT])
        tokno = sb(gs, "tokno", [P, L], I32)
        bn = sb(gs, "bn2", [P, L, 6])
        v2 = sb(gs, "v2", [P, NW])
        t2 = sb(gs, "t2", [P, NW])
        xn4 = sb(gs, "xn4", [P, 2, TG, D])
        hTh = sb(gs, "hTh", [P, 2, TG // 2 * PB * P], F16)
        hTl = sb(gs, "hTl", [P, 2, TG // 2 * PB * P], F16)
        lg = (xn4[:, :, :, :].rearrange("p s i c -> p (s i c)")[:, 0:(NW + NW % 2) * E]
              .rearrange("p (t e) -> p t e", e=E))
        oh = [sb(gs, f"oh{w}", [P, E, n], F16) for w, n in enumerate(WAVES)]
        pos = sb(gs, "pos", [P, E, NW])
        mx = sb(gs, "mx", [P, NW])
        cnt = sb(gs, "cnt", [P, 8 * E])
        gate_stack.close()
        w2s = sb(st, "w2s", [P, 2, W2F], F16)

        at = [0]

        def take(shape, dt=F32, parts=P):
            n = math.prod(shape) * (1 if dt != F16 else 2) // (1 if dt != F16 else 4)
            v = Hflat[0:parts, at[0]:at[0] + n]
            at[0] += n
            assert at[0] <= WAVES[0] * ROW
            if dt != F32:
                v = v.bitcast(dt)
            names = "abcd"[:len(shape)]
            return v.rearrange(f"p ({' '.join(names)}) -> p {' '.join(names)}", **dict(zip(names[1:], shape[1:])))

        xt = take([4, 2, ROW])
        xn = take([2, 2, D])
        xT = take([2, 2 * TS], F16)
        xTl = take([2, TS], F16)
        gel = take([NB, TS])
        gh = take([2, NB, TS], F16)
        gl = take([2, NB, TS], F16)
        z = take([2, 2, ROW])
        zi = [take([2]).bitcast(I32) for s in range(2)]

        ps = st.enter_context(nc.psum_tensor("cps", [P, 8, 512], F32))

        cc, w1_in, w2_in, sorted0, sorted1 = (sem(s) for s in ("c_consts", "w1_in", "w2_in", "sorted0", "sorted1"))
        g_bn, g_sqrt, g_norm, g_norm_pool, g_norm_dve, g_scaled, g_turn, g_high, g_low, g_logit, g_step, wg_high, wg_low = (
            sem(s) for s in ("g_bn", "g_sqrt", "g_norm", "g_norm_pool", "g_norm_dve", "g_scaled", "g_turn",
                             "g_high", "g_low", "g_logit",
                             "g_step", "wg_high", "wg_low"))
        ready = [sem(f"dest_ready{w}") for w in range(2)]
        oh_ready, cnt_ready, stats_ready = sem("oh_ready"), sem("cnt_ready"), sem("stats_ready")
        x_in = [sem(f"x_in{s}") for s in range(4)]
        scattered = [sem(f"scattered{s}") for s in range(2)]
        (xn_ready, xT_turned, xT_high, xT_low, g1_done, gel_done, gh_done, gs_done, y_done, z_done, o_done,
         zi_done) = (
            sem(s) for s in ("xn_ready", "xT_turned", "xT_high", "xT_low", "g1_done", "gel_done", "gh_done",
                             "gs_done", "y_done", "z_done", "o_done", "zi_done"))
        block = st.enter_context(nc.Block())

        def turned_tokens(s):
            return ps[:, 2 * s:2 * s + 2, :].rearrange("p a b -> p (a b)")[:, 0:TG // 2 * PB * P]

        def token_row(g, i, w):
            t = TG * (g - sum(GROUPS[:w])) + sum(WAVES[:w]) + i
            return H[:, bass.ds(t, 1), :].rearrange("p o c -> p (o c)")

        def expert_of(eng, i):
            return eng.value_load(experts[0:1, bass.ds(i, 1)]).with_bounds(min_val=0, max_val=E - 1)

        def x_rows(i):
            return rows[bass.ds(TS * i, TS), :].rearrange("(p j) c -> p (j c)", j=2)

        def send(pool, w, n0, n1):
            for n in range(n0, n1):
                t = n - WAVES[w]
                source, place = ((H[:, sum(WAVES[:w]) + n, :], dest[w][:, n:n + 1]) if t < 0 else
                                 (padrow[:, :], paddest[w][:, t:t + 1]))
                pool.indirect_dma_start(out=rows, out_offset=bass.IndirectOffsetOnAxis(ap=place, axis=0),
                                        in_=source, in_offset=None, bounds_check=NT * TS - 1,
                                        oob_is_err=False).then_inc((sorted0, sorted1)[w], 16)

        @block.sync
        def _(sp):
            for dst, src in ((wg_raw[:, :, :], w_gate),
                             (bg2[:, :], b_gate.partition_broadcast(P)), (triu_raw[:, :], triu_d),
                             (padno[:, :], padno_d), (tileno[:, :], tileno_d), (tokno[:, :], tokno_d),
                             (b1s[:, :], b1c),
                             (b2s[:, :, :].rearrange("p e c -> p (e c)"),
                              b2.rearrange("e c -> (e c)").partition_broadcast(P))):
                sp.dma_start(dst, src).then_inc(cc, 16)
            for h in range(2):
                sp.dma_start(w1s[:, h, :], wsplit[:, h * WF:h * WF + 2 * W1F]).then_inc(w1_in, 16)
            def load(i, s):
                wait(sp, xn_ready, i - 3)
                wait(sp, z_done, i - 3)
                sp.dma_start(xt[:, s, :, :].rearrange("p j c -> p (j c)"), x_rows(i)).then_inc(x_in[s], 16)

            n0 = WAVE_TILES[0]
            sp.wait_ge(sorted0, 16 * 2 * WAVE_TILES[0])
            for i in range(4):
                if i == 3:
                    sp.wait_ge(ready[1], 1)
                    for h in range(2):
                        sp.dma_start(w2s[:, h, :], wsplit[:, h * WF + 2 * W1F:(h + 1) * WF]).then_inc(w2_in, 16)
                load(i, i)
            with sp.Fori(1, n0 // 4) as it:
                for s in range(4):
                    load(4 * it + s, s)
            sp.wait_ge(sorted1, 16 * 2 * WAVE_TILES[1])
            with sp.Fori(n0 // 4, NT // 4) as it:
                for s in range(4):
                    load(4 * it + s, s)
            for i in range(NT // 4 * 4, NT):
                load(i, i % 4)

        @block.vector
        def _(dve):
            n = [0]

            def step(ins):
                ins.then_inc(g_step, 1)
                n[0] += 1
                dve.wait_ge(g_step, n[0])

            def stats(t):
                dve.bn_stats(bn[:, bass.ds(t, 1), :].rearrange("p o s -> p (o s)"),
                             H[:, bass.ds(t, 1), 0:D].rearrange("p o c -> p (o c)")).then_inc(g_bn, 1)

            with dve.Fori(0, WAVES[0] // 20) as it:
                for i in range(20):
                    stats(20 * it + i)
            for t in range(WAVES[0] // 20 * 20, WAVES[0]):
                stats(t)

            t0, tile0 = 0, 0
            for w, nw in enumerate(WAVES):
                nt = WAVE_TILES[w]
                if w == 1:
                    for t in range(WAVES[0] + AHEAD * GROUPS[0], L):
                        stats(t)
                dve.wait_ge(g_bn, t0 + nw)
                mean, var = H[:, t0:t0 + nw, STAT0], H[:, t0:t0 + nw, STAT1]
                v, t_, r = v2[:, 0:nw], t2[:, 0:nw], mx[:, 0:nw]
                m_even, s_even, m_odd, s_odd = (bn[:, t0:t0 + nw, c] for c in (1, 2, 4, 5))
                step(dve.tensor_tensor(t_, m_even, m_odd, ALU.subtract))
                step(dve.scalar_tensor_tensor(t_, t_, 0.25 * D, t_, ALU.mult, ALU.mult))
                step(dve.tensor_tensor(v, s_even, s_odd, ALU.add))
                step(dve.tensor_tensor(v, v, t_, ALU.add))
                step(dve.tensor_tensor(mean, m_even, m_odd, ALU.add))
                step(dve.tensor_scalar(mean, mean, 0.5, None, ALU.mult))
                dve.tensor_scalar(v, v, 1.0 / D, EPS, ALU.mult, ALU.add).then_inc(stats_ready, 1)
                if w == 0:
                    dve.wait_ge(cc, 16 * 8)
                    step(dve.memset(padrow[:, :], 0.0))
                    step(dve.tensor_scalar(padrow[:, TOKEN:TOKEN + 1].bitcast(I32), padrow[:, 0:1], float(NOWHERE), None,
                                           ALU.add))
                    step(dve.memset(ones[:, :], 1.0))
                    step(dve.memset(ones16[:, :], 1.0))
                    step(dve.tensor_copy(triu[:, :], triu_raw[:, :]))
                    step(dve.tensor_copy(H[:, :, TOKEN].bitcast(I32), tokno[:, :]))
                    dve.wait_ge(wg_high, 1)
                    dve.scalar_tensor_tensor(wg[:, :, 1, :], wg_raw[:, :, :], WSCALE, wg[:, :, 0, :], ALU.mult,
                                             ALU.subtract).then_inc(wg_low, 1)
                dve.wait_ge(g_sqrt, w + 1)
                step(dve.reciprocal(r, t_))
                step(dve.tensor_tensor(t_, r, r, ALU.mult))
                step(dve.tensor_tensor(t_, t_, v, ALU.mult))
                step(dve.tensor_scalar(t_, t_, -0.5, 1.5, ALU.mult, ALU.add))
                step(dve.tensor_tensor(r, r, t_, ALU.mult))
                step(dve.tensor_tensor(t_, mean, r, ALU.mult))
                step(dve.tensor_scalar(var, t_, -1.0, None, ALU.mult))
                dve.tensor_copy(mean, r).then_inc(stats_ready, 1)

                def group(g, s, k, ahead, w=w):
                    if w == 1 and ahead:
                        normalise(g + 1, 1 - s, ahead)
                    dve.wait_ge(g_high, g + 1)
                    wait(dve, g_logit, g - 1)
                    dve.tensor_tensor(hTl[:, s, :], turned_tokens(s), hTh[:, s, :], ALU.subtract).then_inc(g_low, 1)
                    if w == 0:
                        for i in range(AHEAD):
                            stats(AHEAD * g + WAVES[0] + i)

                def normalise(g, s, k=TG):
                    wait(dve, g_turn, g - 1)
                    for i in range(BY_ACT[1], k):
                        row = token_row(g, i, 1)
                        a = dve.tensor_scalar(xn4[:, s, i, :], row[:, 0:D], row[:, STAT0:STAT0 + 1],
                                              row[:, STAT1:STAT1 + 1], ALU.mult, ALU.add)
                    a.then_inc(g_norm_dve, 1)

                if w == 1:
                    dve.wait_ge(stats_ready, 4)
                    normalise(GROUPS[0], GROUPS[0] % 2)
                gate_groups(dve, w, group)

                dve.wait_ge(g_logit, sum(GROUPS[:w + 1]))
                lw, np_ = lg[:, 0:nw, :], (nw + 1) // 2
                parts = (ps[:, 4:6, :].rearrange("p a b -> p (a b)")[:, 0:4 * E * np_]
                         .rearrange("p (t h e) -> p t h e", h=2, e=2 * E))
                lp = lg[:, 0:2 * np_, :].rearrange("p (t s) e -> p t (s e)", s=2)
                bias = bg2[:, :].rearrange("p (o e) -> p o e", o=1).to_broadcast([P, np_, 2 * E])
                step(dve.scalar_tensor_tensor(lp, parts[:, :, 0, :], 1 / WSCALE, bias, ALU.mult, ALU.add))
                step(dve.scalar_tensor_tensor(lp, parts[:, :, 1, :], 1 / WSCALE, lp, ALU.mult, ALU.add))
                step(dve.tensor_reduce(mx[:, 0:nw], lw, AX_X, ALU.max))
                step(dve.tensor_tensor(lw, lw, mx[:, 0:nw].rearrange("p (t o) -> p t o", o=1).to_broadcast([P, nw, E]),
                                       ALU.is_ge))
                step(dve.tensor_copy(oh[w][:, 0, :], lw[:, :, 0]))
                step(dve.tensor_copy(mx[:, 0:nw], lw[:, :, 0]))
                for e in range(1, E - 1):
                    step(dve.tensor_tensor(oh[w][:, e, :], lw[:, :, e], mx[:, 0:nw], ALU.is_gt))
                    step(dve.tensor_tensor(mx[:, 0:nw], lw[:, :, e], mx[:, 0:nw], ALU.max))
                dve.tensor_tensor(oh[w][:, E - 1, :], lw[:, :, E - 1], mx[:, 0:nw], ALU.is_gt).then_inc(oh_ready, 1)

                dve.wait_ge(cnt_ready, w + 1)
                before, column = (ps[:, b, 0:E * nw].rearrange("p (e t) -> p e t", e=E) for b in (4, 6))
                for e in range(E):
                    step(dve.tensor_tensor_scan(pos[:, e, 0:nw], ones[:, 0:nw], column[:, e, :], 0.0, ALU.mult, ALU.add))
                tot, size, end, base, gap, pad_at = (cnt[:, E * k:E * k + E] for k in range(6))
                step(dve.tensor_copy(tot, pos[:, :, nw - 1]))
                step(dve.tensor_scalar(size, tot, 1.0 / TS, (TS - 1.0) / TS - 0.5 + 0.5 / TS, ALU.mult, ALU.add))
                step(dve.tensor_scalar(size, size, MAGIC, None, ALU.add))
                step(dve.tensor_scalar(size, size, MAGIC, float(TS), ALU.subtract, ALU.mult))
                step(dve.tensor_tensor_scan(end, ones[:, 0:E], size, 0.0, ALU.mult, ALU.add))
                step(dve.tensor_tensor(base, end, size, ALU.subtract))
                step(dve.tensor_tensor(gap, size, tot, ALU.subtract))
                step(dve.tensor_tensor_scan(pad_at, ones[:, 0:E], gap, 0.0, ALU.mult, ALU.add))
                pw = pos[:, :, 0:nw]
                step(dve.tensor_tensor(pw, pw, column, ALU.subtract))
                step(dve.tensor_tensor(pw, before, pw, ALU.add))
                step(dve.tensor_tensor(pw, pw, base.rearrange("p (e o) -> p e o", o=1).to_broadcast([P, E, nw]), ALU.add))
                step(dve.tensor_tensor(pw, pw, oh[w][:, :, :], ALU.mult))
                step(dve.tensor_reduce(v, pw.rearrange("p e t -> p t e"), AX_X, ALU.add))
                step(dve.tensor_scalar(dest[w][:, :], v, float(TS * tile0), None, ALU.add))
                step(dve.tensor_scalar(padpos[:, :], padno[:, :], tot[:, 0:1], None, ALU.add))
                for e in range(1, E):
                    step(dve.tensor_scalar(padt[:, :], padno[:, :], pad_at[:, e - 1:e], tot[:, e:e + 1], ALU.is_ge,
                                           ALU.mult))
                    step(dve.tensor_tensor(padpos[:, :], padpos[:, :], padt[:, :], ALU.add))
                step(dve.tensor_scalar(paddest[w][:, :], padpos[:, :], float(TS * tile0), None, ALU.add))
                te, tt, tn = (a[:, tile0:tile0 + nt] for a in (tilee, tilet, tileno))
                step(dve.tensor_scalar(te, tn, base[0:1, 1:2], None, ALU.is_ge))
                for e in range(2, E):
                    step(dve.tensor_scalar(tt, tn, base[0:1, e:e + 1], None, ALU.is_ge))
                    step(dve.tensor_tensor(te, te, tt, ALU.add))
                dve.tensor_copy(experts[:, tile0:tile0 + nt], te).then_inc(ready[w], 1)
                dve.wait_ge(ready[w], 1)
                t0 += nw
                tile0 += nt

            def split_x(i, s):
                dve.wait_ge(xT_high, i + 1)
                dve.tensor_tensor(xTl[:, s, :], ps[:, 7, 0:TS], xT[:, s, 0:TS], ALU.subtract).then_inc(xT_low, 1)
                dve.tensor_tensor(xT[0:LOW, s, TS:2 * TS], ps[LOW:P, 7, TS:2 * TS], xT[LOW:P, s, TS:2 * TS],
                                  ALU.subtract).then_inc(xT_low, 1)

            def split_h(i, s, b):
                dve.wait_ge(gel_done, NB * i + b + 2)
                wait(dve, y_done, i - 1)
                dve.tensor_copy(gh[:, s, b:b + 2, :], gel[:, b:b + 2, :]).then_inc(gh_done, 1)
                dve.wait_ge(gh_done, NB // 2 * i + b // 2 + 1)
                dve.tensor_tensor(gl[:, s, b:b + 2, :], gel[:, b:b + 2, :], gh[:, s, b:b + 2, :],
                                  ALU.subtract).then_inc(gs_done, 1)

            def output(i, s):
                dve.wait_ge(y_done, i + 1)
                dve.wait_ge(z_done, i + 1)
                dve.scalar_tensor_tensor(z[:, s, :, 0:D], ps[:, 5 + s, :].rearrange("p (j c) -> p j c", j=2)[:, :, 0:D],
                                         1 / WSCALE, z[:, s, :, 0:D], ALU.mult, ALU.add).then_inc(o_done, 1)

            def tile(i, r, it, first=False, last=False):
                split_h(i, r % 2, 0)
                if not last:
                    split_x(i + 1, (r + 1) % 2)
                split_h(i, r % 2, 2)
                split_h(i, r % 2, 4)
                if not first:
                    output(i - 1, (r + 1) % 2)

            split_x(0, 0)
            tile_loop(dve, tile)
            output(NT - 1, (NT - 1) % 2)

        @block.scalar
        def _(act):
            act.wait_ge(cc, 16 * 8)
            act.activation(wg[:, :, 0, :], wg_raw[:, :, :], ACT.Copy, scale=WSCALE).then_inc(wg_high, 1)
            for w, nw in enumerate(WAVES):
                act.wait_ge(stats_ready, 2 * w + 1)
                act.activation(t2[:, 0:nw], v2[:, 0:nw], ACT.Sqrt).then_inc(g_sqrt, 1)
                act.wait_ge(stats_ready, 2 * w + 2)

                def normalise(g, s, k=TG, w=w):
                    wait(act, g_turn, g - 1)
                    for i in range(min(k, BY_ACT[w])):
                        row = token_row(g, i, w)
                        a = act.activation(xn4[:, s, i, :], row[:, 0:D], ACT.Identity, bias=row[:, STAT1:STAT1 + 1],
                                           scale=row[:, STAT0:STAT0 + 1])
                    a.then_inc(g_norm, 1)

                def group(g, s, k, ahead):
                    if ahead:
                        normalise(g + 1, 1 - s, ahead)
                    act.wait_ge(g_turn, g + 1)
                    wait(act, g_logit, g - 1)
                    act.activation(hTh[:, s, :], turned_tokens(s), ACT.Copy).then_inc(g_high, 1)

                g0 = sum(GROUPS[:w])
                normalise(g0, g0 % 2)
                gate_groups(act, w, group)

            def norm_x(i, x_slot, s, uses):
                act.wait_ge(x_in[x_slot], 16 * uses)
                wait(act, xT_turned, i - 1)
                for j in range(2):
                    row = xt[:, x_slot, j, :]
                    a = act.activation(xn[:, s, j, :], row[:, 0:D], ACT.Identity, bias=row[:, STAT1:STAT1 + 1],
                                       scale=row[:, STAT0:STAT0 + 1])
                a.then_inc(xn_ready, 1)

            def high_x(i, s):
                act.wait_ge(xT_turned, i + 1)
                wait(act, g1_done, NB * (i - 1))
                act.activation(xT[:, s, :], ps[:, 7, :], ACT.Copy).then_inc(xT_high, 1)

            def gelu(i, b, r, ex):
                bank = (2 * r + b) % 4
                act.wait_ge(g1_done, NB * i + b + 1)
                wait(act, gs_done, NB // 2 * (i - 1) + b // 2 + 1)
                act.activation(gel[:, b, :], ps[:, bank, 0:TS], ACT.Gelu,
                               bias=b1s[:, bass.ds(NB * ex + b, 1)], scale=1 / WSCALE).then_inc(gel_done, 1)

            def tile(i, r, it, first=False, last=False):
                ex = expert_of(act, i)
                for b in range(NB):
                    gelu(i, b, r, ex)
                    if b == 1 and not last:
                        high_x(i + 1, (r + 1) % 2)
                    if b == 4 and not (isinstance(i, int) and i + 2 >= NT):
                        norm_x(i + 2, (r + 2) % 4, r % 2, it + (r + 2) // 4 + 1)

            norm_x(0, 0, 0, 1)
            norm_x(1, 1, 1, 1)
            act.wait_ge(ready[1], 1)
            high_x(0, 0)
            tile_loop(act, tile)

        @block.tensor
        def _(pe):
            pe.wait_ge(cc, 16 * 8)
            pe.wait_ge(wg_low, 1)
            for w, nw in enumerate(WAVES):
                def turn(g, s, k=TG, w=w):
                    pe.wait_ge(g_norm, g + 1)
                    if k > BY_ACT[w]:
                        pe.wait_ge((g_norm_pool, g_norm_dve)[w], g - sum(GROUPS[:w]) + 1)
                    wait(pe, g_low, g - 1)
                    for i in range((k + 1) // 2 * PB):
                        mm = pe.transpose(turned_tokens(s)[:, i * P:(i + 1) * P],
                                          xn4[:, s, :, :].rearrange("p i c -> p (i c)")[:, i * P:(i + 1) * P], ident[:, :])
                    mm.then_inc(g_turn, 1)

                def logits(g, s, k=TG, w=w):
                    pe.wait_ge(g_low, g + 1)
                    tb = TG * (g - sum(GROUPS[:w]))
                    psl = ps[:, 4:6, :].rearrange("p a b -> p (a b)")
                    for i in range((k + 1) // 2 * PB):
                        blk, n, c = slice(i * P, (i + 1) * P), i % PB, 2 * E * tb + 4 * E * (i // PB)
                        pe.matmul(psl[:, bass.ds(c, 4 * E)], hTh[:, s, blk], wg[:, n, :, :].rearrange("p h e -> p (h e)"),
                                  start=(n == 0), stop=False, skip_group_check=True)
                        mm = pe.matmul(psl[:, bass.ds(c, 2 * E)], hTl[:, s, blk], wg[:, n, 0, :],
                                       start=False, stop=(n == PB - 1), skip_group_check=True)
                    mm.then_inc(g_logit, 1)

                g0 = sum(GROUPS[:w])
                if w:
                    pe.wait_ge(ready[w - 1], 1)
                def group(g, s, k, ahead):
                    if ahead:
                        turn(g + 1, 1 - s, ahead)
                    logits(g, s, k)

                turn(g0, g0 % 2)
                gate_groups(pe, w, group)
                pe.wait_ge(oh_ready, w + 1)
                hot = oh[w][:, :, :].rearrange("p e t -> p (e t)")
                pe.matmul(ps[:, 4, 0:E * nw], triu[:, :], hot, start=True, stop=True, skip_group_check=True)
                pe.matmul(ps[:, 6, 0:E * nw], ones16[:, :], hot, start=True, stop=True,
                          skip_group_check=True).then_inc(cnt_ready, 1)

            pe.wait_ge(ready[1], 1)
            pe.wait_ge(w1_in, 32)

            def turn_x(i, s):
                pe.wait_ge(xn_ready, i + 1)
                wait(pe, xT_low, 2 * i)
                for j in range(2):
                    pe.transpose(ps[:, 7, j * P:(j + 1) * P], xn[:, s, j, 0:P], ident[:, :])
                    mm = pe.transpose(ps[:, 7, TS + j * P:TS + (j + 1) * P], xn[:, s, j, LOW:D], ident[:, :])
                mm.then_inc(xT_turned, 1)

            def layer1(i, b, r, s, ex):
                bank = (2 * r + b) % 4
                wait(pe, gel_done, NB * i + b - 3)
                o = ps[:, bank, 0:TS]
                for n, (h, part, mov) in enumerate(((0, 0, xT[:, s, 0:TS]), (1, 0, xT[:, s, 0:TS]), (0, 0, xTl[:, s, :]),
                                                    (0, 1, xT[:, s, TS:2 * TS]), (1, 1, xT[:, s, TS:2 * TS]))):
                    mm = pe.matmul(o, w1s[:, h, bass.ds(ex * HID + part * W1F + b * P, P)], mov,
                                   start=(n == 0), stop=(n == 4))
                mm.then_inc(g1_done, 1)

            def layer2(i, b, s, ex):
                if b == 0:
                    if isinstance(i, int) and i == 0:
                        pe.wait_ge(w2_in, 32)
                    wait(pe, o_done, i - 1)
                if b % 2 == 0:
                    pe.wait_ge(gs_done, NB // 2 * i + b // 2 + 1)
                for j in range(2):
                    t = slice(j * P, (j + 1) * P)
                    o = ps[:, 5 + s, j * TS:j * TS + D]
                    for n, (g, h) in enumerate(((gh, 0), (gh, 1), (gl, 0))):
                        mm = pe.matmul(o, g[:, s, b, t], w2s[:, h, bass.ds(ex * (NB * D) + b * D, D)],
                                       start=(b == 0 and j == 0 and n == 0), stop=(b == NB - 1 and n == 2),
                                       skip_group_check=True)
                if b == NB - 1:
                    mm.then_inc(y_done, 1)

            def tile(i, r, it, first=False, last=False):
                ex, prev = carried if r else (expert_of(pe, i), None)
                for b in range(NB):
                    layer1(i, b, r, r % 2, ex)
                    if r == 0 and b == 0 and not first:
                        prev = expert_of(pe, i - 1)
                    if b == 4 and not last:
                        pe.wait_ge(xT_low, 2 * i + 4)
                    if not first:
                        layer2(i - 1, b, (r + 1) % 2, prev)
                    if b == 1 and not last:
                        turn_x(i + 1, (r + 1) % 2)
                        if r < 3:
                            carried[:] = expert_of(pe, i + 1), ex

            carried = [None, None]
            turn_x(0, 0)
            pe.wait_ge(xT_low, 2)
            tile_loop(pe, tile)
            prev = expert_of(pe, NT - 1)
            for b in range(NB):
                layer2(NT - 1, b, (NT - 1) % 2, prev)

        @block.gpsimd
        def _(pool):
            def normalise(g, s, k=TG):
                waits(pool, (stats_ready, 2), (g_turn, g - 1))
                for i in range(BY_ACT[0], k):
                    row = token_row(g, i, 0)
                    pool.tensor_tensor(xn4[:, s, i, :], row[:, 0:D], row[:, STAT0:STAT0 + 1].to_broadcast([P, D]),
                                       ALU.mult).then_inc(g_scaled, 1)
                    waits(pool, (stats_ready, 2), (g_scaled, (TG - BY_ACT[0]) * g + i - BY_ACT[0] + 1))
                    a = pool.tensor_tensor(xn4[:, s, i, :], xn4[:, s, i, :], row[:, STAT1:STAT1 + 1].to_broadcast([P, D]),
                                           ALU.add)
                a.then_inc(g_norm_pool, 1)

            def group(g, s, k, ahead):
                if ahead > BY_ACT[0]:
                    normalise(g + 1, 1 - s, ahead)

            normalise(0, 0)
            gate_groups(pool, 0, group)
            pool.wait_ge(ready[0], 1)
            send(pool, 0, 0, 2 * WAVE_TILES[0])

            def residual(i, x_slot, s, uses):
                ex = expert_of(pool, i)
                waits(pool, (ready[1], 1), (x_in[x_slot], 16 * uses), (scattered[s], uses_scatter(i, s)))
                bias = b2s[:, bass.ds(ex, 1), :].to_broadcast([P, 2, D])
                pool.tensor_copy(zi[s], xt[:, x_slot, :, TOKEN].bitcast(I32)).then_inc(zi_done, 1)
                pool.tensor_tensor(z[:, s, :, 0:D], xt[:, x_slot, :, 0:D], bias, ALU.add).then_inc(z_done, 1)

            def uses_scatter(i, s):
                return 32 * (i // 2) if isinstance(i, int) else 16 * (i - s)

            def store(i, s):
                waits(pool, (ready[1], 1), (o_done, i + 1), (zi_done, i + 1))
                for j in range(2):
                    pool.indirect_dma_start(out=out_rows, out_offset=bass.IndirectOffsetOnAxis(ap=zi[s][:, j:j + 1], axis=0),
                                            in_=z[:, s, j, 0:D], in_offset=None, bounds_check=B * L - 1,
                                            oob_is_err=False).then_inc(scattered[s], 16)

            def tile(i, r, it, first=False, last=False):
                residual(i, r, r % 2, it + 1)
                if not first:
                    store(i - 1, (r + 1) % 2)

            def sent(tiles):
                n = 2 * WAVE_TILES[1]
                return min(n, SEND_FIRST + (n - SEND_FIRST) * tiles // (WAVE_TILES[0] - 4)) if tiles else 0

            for i in range(WAVE_TILES[0]):
                tile(i, i % 4, i // 4, first=i == 0)
                send(pool, 1, sent(i), sent(i + 1))
            with pool.Fori(WAVE_TILES[0] // 4, NT // 4) as it:
                for r in range(4):
                    tile(4 * it + r, r, it)
            for i in range(NT // 4 * 4, NT):
                tile(i, i % 4, i // 4)
            store(NT - 1, (NT - 1) % 2)
            for s in range(2):
                pool.wait_ge(scattered[s], 32 * ((NT - s + 1) // 2))



def kernel(x, cls_tok, L0_tok_W_proj, L0_tok_b_proj, L0_attn_w1, L0_attn_b1, L0_attn_w2, L0_attn_b2, L0_attn_w3,
           L0_attn_b3, L0_attn_freq, L0_attn_deltas_abs, L0_attn_bias, L0_ffn_Wg, L0_ffn_bg, L0_ffn_W1, L0_ffn_b1,
           L0_ffn_W2, L0_ffn_b2):
    import numpy as np
    import concourse.bacc as bacc
    from concourse.bass_utils import run_bass_kernel_spmd

    def a(v):
        return np.ascontiguousarray(v)

    t = np.linspace(0.0, 1.0, L, dtype=np.float32)
    w = (np.float32(2 * np.pi) * np.linspace(0.0, float(L - 1), L, dtype=np.float32) / np.float32(L)).astype(np.float32)
    fw = np.float32(0.0001) * w
    z = np.stack([t, np.cos(fw), -np.sin(fw)]).astype(np.float32)
    p = np.arange(P)

    wg_pair = np.zeros((2, D, 2, E), np.float32)
    wg_pair[0, :, 0], wg_pair[1, :, 1] = L0_ffn_Wg, L0_ffn_Wg
    wg_pair = a(wg_pair.reshape(PB, P, 2 * E).transpose(1, 0, 2))

    arrays = {
        "x": a(x), "cls_tok": a(cls_tok).reshape(D),
        "wprojT": a(a(L0_tok_W_proj).T), "b_proj": a(L0_tok_b_proj),
        "zT": a(z), "trow": t,
        "fw1T": a(a(L0_attn_w1).T), "fw2T": a(a(L0_attn_w2).T), "fw3T": a(a(L0_attn_w3).T),
        "fcols": a(np.stack([a(L0_attn_b1), a(L0_attn_b2), a(L0_attn_freq), a(L0_attn_freq)], axis=1)),
        "f3cols": a(np.concatenate([a(v).reshape(2, 96).T for v in (L0_attn_b3, L0_attn_deltas_abs, L0_attn_bias)], axis=1)),
        "w_gate": wg_pair, "b_gate": a(np.concatenate([L0_ffn_bg, L0_ffn_bg])),
        "w1": a(L0_ffn_W1), "b1c": a(a(L0_ffn_b1).reshape(E * NB, P).T),
        "w2": a(L0_ffn_W2), "b2": a(L0_ffn_b2),
        "ident_d": np.eye(P, dtype=np.float32),
        "triu_d": np.triu(np.ones((P, P), np.float32), 1),
        "tokno_d": a((p[:, None] * L + np.arange(L)[None]).astype(np.int32)),
        "padno_d": a((np.arange(8)[None] * P + p[:, None]).astype(np.float32)),
        "tileno_d": np.concatenate([np.arange(n) * TS for n in WAVE_TILES]).astype(np.float32)[None],
    }
    nc = bacc.Bacc("TRN2", target_bir_lowering=False, num_devices=1)
    args = {n: nc.dram_tensor(n, v.shape, mybir.dt.from_np(v.dtype), kind="ExternalInput").ap() for n, v in arrays.items()}
    out = nc.dram_tensor("out", (B, L, D), F32, kind="ExternalOutput").ap()
    vit_block(nc, **args, out=out)
    return run_bass_kernel_spmd(nc, [arrays], core_ids=[0]).results[0]["out"]
```
